# Optimizing a Trainium2 kernel written in Bass

```python
import numpy as np
import jax
import jax.numpy as jnp

def _softmax(x, axis=-1):
    return jax.nn.softmax(x, axis=axis)

def _gelu(x):
    return jax.nn.gelu(x, approximate=True)

def _silu(x):
    return jax.nn.silu(x)

def _sigmoid(x):
    return jax.nn.sigmoid(x)

def _layernorm(x, axis=-1, eps=1e-05):
    m = jnp.mean(x, axis=axis, keepdims=True)
    v = jnp.var(x, axis=axis, keepdims=True)
    return (x - m) / jnp.sqrt(v + eps)

def _scatter_add(tgt, idx, src, axis=0):
    return tgt.at[idx].add(src)

def _segment_sum(src, seg, n):
    return jax.ops.segment_sum(src, seg, n)
kernel_name = 'mk_prb_d1_jaxref_r8_3ebd5c'

def setup_inputs(seed: int=0):
    np.random.seed(seed)
    _w = jnp.asarray

    def _L0_attn_setup():
        import jax, jax.numpy as jnp
        import numpy as np
        E = 128
        H = 16
        HD = E // H
        MAX_REL = 20
        key = jax.random.key(seed)
        ks = jax.random.split(key, 12)
        B, S = (4, 128)

        def lin_w(k):
            return jax.random.normal(k, (E, E), dtype=jnp.float32) * (1.0 / np.sqrt(E))
        return {'hidden_states': jax.random.normal(ks[0], (B, S, E), dtype=jnp.float32), 'Wq': lin_w(ks[1]), 'bq': jnp.zeros((E,), jnp.float32), 'Wk': lin_w(ks[2]), 'bk': jnp.zeros((E,), jnp.float32), 'Wv': lin_w(ks[3]), 'bv': jnp.zeros((E,), jnp.float32), 'Wo': lin_w(ks[4]), 'bo': jnp.zeros((E,), jnp.float32), 'rel_k': jax.random.uniform(ks[5], (2 * MAX_REL + 1, HD), jnp.float32, -0.24, 0.24), 'rel_v': jax.random.uniform(ks[6], (2 * MAX_REL + 1, HD), jnp.float32, -0.24, 0.24)}
    _L0_attn_in = _L0_attn_setup()

    def _L0_ffn_setup():
        import jax, jax.numpy as jnp
        import numpy as np
        D_MODEL = 128
        NUM_HEADS = 4
        NUM_EXPERTS = 8
        TOP_K = 2
        D_FF = 128
        EPS = 1e-06

        def _rmsnorm(x, g):
            return x * jax.lax.rsqrt(jnp.mean(x * x, axis=-1, keepdims=True) + EPS) * g

        def _swiglu(x, w1, w2, w3):
            return jax.nn.silu(x @ w1.T) * (x @ w3.T) @ w2.T
        key = jax.random.key(seed)
        ks = jax.random.split(key, 16)
        d, e, f = (D_MODEL, NUM_EXPERTS, D_FF)
        dc = d // 4
        s = 0.02
        return {'X': jax.random.normal(ks[0], (2, 128, d), dtype=jnp.float32), 'g1': jnp.ones((d,), jnp.float32), 'g2': jnp.ones((d,), jnp.float32), 'Wq': jax.random.normal(ks[1], (d, d), jnp.float32) * s, 'Wkc': jax.random.normal(ks[2], (dc, d), jnp.float32) * s, 'Wvc': jax.random.normal(ks[3], (dc, d), jnp.float32) * s, 'Wo': jax.random.normal(ks[4], (d, d), jnp.float32) * s, 'Wr': jax.random.normal(ks[5], (e, d), jnp.float32) * s, 'expert_bias': jnp.zeros((e,), jnp.float32), 'sW1': jax.random.normal(ks[6], (f, d), jnp.float32) * s, 'sW2': jax.random.normal(ks[7], (d, f), jnp.float32) * s, 'sW3': jax.random.normal(ks[8], (f, d), jnp.float32) * s, 'eW1': jax.random.normal(ks[9], (e, f, d), jnp.float32) * s, 'eW2': jax.random.normal(ks[10], (e, d, f), jnp.float32) * s, 'eW3': jax.random.normal(ks[11], (e, f, d), jnp.float32) * s}
    _L0_ffn_in = _L0_ffn_setup()
    _d = {'L0_attn_hidden_states': _L0_attn_in['hidden_states'], 'L0_attn_Wq': _L0_attn_in['Wq'], 'L0_attn_bq': _L0_attn_in['bq'], 'L0_attn_Wk': _L0_attn_in['Wk'], 'L0_attn_bk': _L0_attn_in['bk'], 'L0_attn_Wv': _L0_attn_in['Wv'], 'L0_attn_bv': _L0_attn_in['bv'], 'L0_attn_Wo': _L0_attn_in['Wo'], 'L0_attn_bo': _L0_attn_in['bo'], 'L0_attn_rel_k': _L0_attn_in['rel_k'], 'L0_attn_rel_v': _L0_attn_in['rel_v'], 'L0_ffn_g1': _L0_ffn_in['g1'], 'L0_ffn_g2': _L0_ffn_in['g2'], 'L0_ffn_Wq': _L0_ffn_in['Wq'], 'L0_ffn_Wkc': _L0_ffn_in['Wkc'], 'L0_ffn_Wvc': _L0_ffn_in['Wvc'], 'L0_ffn_Wo': _L0_ffn_in['Wo'], 'L0_ffn_Wr': _L0_ffn_in['Wr'], 'L0_ffn_expert_bias': _L0_ffn_in['expert_bias'], 'L0_ffn_sW1': _L0_ffn_in['sW1'], 'L0_ffn_sW2': _L0_ffn_in['sW2'], 'L0_ffn_sW3': _L0_ffn_in['sW3'], 'L0_ffn_eW1': _L0_ffn_in['eW1'], 'L0_ffn_eW2': _L0_ffn_in['eW2'], 'L0_ffn_eW3': _L0_ffn_in['eW3']}
    _x0 = _d['L0_attn_hidden_states']
    _d['L0_attn_hidden_states'] = jax.random.normal(jax.random.fold_in(jax.random.key(seed), 1), (16, 512, 128), dtype=_x0.dtype)
    del _x0
    return _d

def reference(L0_attn_hidden_states, L0_attn_Wq, L0_attn_bq, L0_attn_Wk, L0_attn_bk, L0_attn_Wv, L0_attn_bv, L0_attn_Wo, L0_attn_bo, L0_attn_rel_k, L0_attn_rel_v, L0_ffn_g1, L0_ffn_g2, L0_ffn_Wq, L0_ffn_Wkc, L0_ffn_Wvc, L0_ffn_Wo, L0_ffn_Wr, L0_ffn_expert_bias, L0_ffn_sW1, L0_ffn_sW2, L0_ffn_sW3, L0_ffn_eW1, L0_ffn_eW2, L0_ffn_eW3):

    def _L0_attn_ref(hidden_states, Wq, bq, Wk, bk, Wv, bv, Wo, bo, rel_k, rel_v):
        import jax, jax.numpy as jnp
        import numpy as np
        E = 128
        H = 16
        HD = E // H
        MAX_REL = 20
        B, S, _ = hidden_states.shape
        scale = jnp.sqrt(jnp.float32(HD))

        def proj(W, b):
            return (hidden_states @ W.T + b).reshape(B, S, H, HD).transpose(0, 2, 1, 3)
        q = proj(Wq, bq)
        k = proj(Wk, bk)
        v = proj(Wv, bv)
        pos = jnp.arange(S)
        idx = jnp.clip(pos[None, :] - pos[:, None], -MAX_REL, MAX_REL) + MAX_REL
        rk2 = rel_k[idx]
        rv2 = rel_v[idx]
        attn1 = jnp.einsum('bhqd,bhkd->bhqk', q, k)
        attn2 = jnp.einsum('bhqd,qkd->bhqk', q, rk2)
        attn = jax.nn.softmax((attn1 + attn2) / scale, axis=-1)
        w1 = jnp.einsum('bhqk,bhkd->bhqd', attn, v)
        w2 = jnp.einsum('bhqk,qkd->bhqd', attn, rv2)
        x = (w1 + w2).transpose(0, 2, 1, 3).reshape(B, S, E)
        out = x @ Wo.T + bo
        return out

    def _L0_ffn_ref(X, g1, g2, Wq, Wkc, Wvc, Wo, Wr, expert_bias, sW1, sW2, sW3, eW1, eW2, eW3):
        import jax, jax.numpy as jnp
        import numpy as np
        D_MODEL = 128
        NUM_HEADS = 4
        NUM_EXPERTS = 8
        TOP_K = 2
        D_FF = 128
        EPS = 1e-06

        def _rmsnorm(x, g):
            return x * jax.lax.rsqrt(jnp.mean(x * x, axis=-1, keepdims=True) + EPS) * g

        def _swiglu(x, w1, w2, w3):
            return jax.nn.silu(x @ w1.T) * (x @ w3.T) @ w2.T
        B, S, d = X.shape
        H = NUM_HEADS
        dk = d // H
        scale = 1.0 / jnp.sqrt(jnp.float32(dk))
        nx = _rmsnorm(X, g1)
        Q = (nx @ Wq.T).reshape(B, S, H, dk).transpose(0, 2, 1, 3)
        Kc = nx @ Wkc.T
        Vc = nx @ Wvc.T
        scores = jnp.einsum('bhsd,btd->bhst', Q, Kc) * scale
        attn = jax.nn.softmax(scores, axis=-1)
        out = jnp.einsum('bhst,btd->bhsd', attn, Vc)
        out = out.transpose(0, 2, 1, 3).reshape(B, S, d) @ Wo.T
        X = X + out
        nx = _rmsnorm(X, g2)
        xf = nx.reshape(-1, d)
        logits = xf @ Wr.T + expert_bias
        rw = jax.nn.softmax(logits, axis=-1)
        topw, topi = jax.lax.top_k(rw, TOP_K)
        topw = jax.nn.softmax(topw, axis=-1)
        combine = jnp.sum(jax.nn.one_hot(topi, NUM_EXPERTS, dtype=xf.dtype) * topw[..., None], axis=1)
        shared = _swiglu(xf, sW1, sW2, sW3)
        h = jax.nn.silu(jnp.einsum('td,efd->etf', xf, eW1)) * jnp.einsum('td,efd->etf', xf, eW3)
        eo = jnp.einsum('etf,edf->etd', h, eW2)
        specialist = jnp.einsum('te,etd->td', combine, eo)
        moe_out = (shared + specialist).reshape(B, S, d)
        return X + moe_out
    x = L0_attn_hidden_states
    xn = _layernorm(x, axis=-1)
    x = x + _L0_attn_ref(xn, L0_attn_Wq, L0_attn_bq, L0_attn_Wk, L0_attn_bk, L0_attn_Wv, L0_attn_bv, L0_attn_Wo, L0_attn_bo, L0_attn_rel_k, L0_attn_rel_v) + _L0_ffn_ref(xn, L0_ffn_g1, L0_ffn_g2, L0_ffn_Wq, L0_ffn_Wkc, L0_ffn_Wvc, L0_ffn_Wo, L0_ffn_Wr, L0_ffn_expert_bias, L0_ffn_sW1, L0_ffn_sW2, L0_ffn_sW3, L0_ffn_eW1, L0_ffn_eW2, L0_ffn_eW3)
    return x

_drawn_inputs = setup_inputs


def setup_inputs(seed=0):
    import zlib

    import numpy as np

    out = dict(_drawn_inputs(seed))
    spreads = {'L0_attn_bq': (0.0, 2.0),
     'L0_attn_bk': (0.0, 2.0),
     'L0_attn_bv': (0.0, 0.8),
     'L0_attn_bo': (0.0, 0.8),
     'L0_ffn_g1': (1.0, 0.6),
     'L0_ffn_g2': (1.0, 0.6),
     'L0_ffn_expert_bias': (0.0, 0.8)}
    factors = {'L0_attn_rel_k': 31.187,
     'L0_ffn_Wq': 8.0,
     'L0_ffn_Wkc': 8.0,
     'L0_ffn_Wvc': 8.0,
     'L0_ffn_Wo': 8.0,
     'L0_ffn_Wr': 8.0,
     'L0_ffn_sW1': 8.0,
     'L0_ffn_sW2': 8.0,
     'L0_ffn_sW3': 8.0,
     'L0_ffn_eW1': 8.0,
     'L0_ffn_eW2': 8.0,
     'L0_ffn_eW3': 8.0,
     'L0_attn_Wq': 3.48,
     'L0_attn_Wk': 3.522,
     'L0_attn_Wv': 3.151,
     'L0_attn_rel_v': 4.935}
    for name, (base, spread) in spreads.items():
        noise = np.random.default_rng([zlib.crc32(name.encode()), seed]).standard_normal(out[name].shape)
        drawn = base * np.exp(spread * noise) if base else spread * noise
        out[name] = jnp.asarray(drawn.astype(out[name].dtype))
    for name, factor in factors.items():
        out[name] = (out[name] * factor).astype(out[name].dtype)
    return out
```

```python
import math
from contextlib import ExitStack

import concourse.bass as bass
from concourse import mybir

F32 = mybir.dt.float32
BF16 = mybir.dt.bfloat16
ALU = mybir.AluOpType
ACT = mybir.ActivationFunctionType
AX = mybir.AxisListType

P = 128
B, S, E = 16, 512, 128
NT = S // P
H, HD = 16, 8
MAX_REL = 20
QBLK = 32
NQB = P // QBLK
FAR = 2 * MAX_REL
WIN = QBLK + FAR
EXT = WIN + QBLK - 1
SLOTS = 6
PARTS = 3
HALF = P // 2
ROWS = SLOTS * HD
G = H // 2
LN_EPS, RMS_EPS = 1e-5, 1e-6
Q_SCALE = HD ** -0.5
Q_PART = (0, 0, 0, 1, 1, 2)
K_PART = (0, 1, 2, 0, 1, 0)


def prepare(nc, x, w, scr, ident_dram):
    with ExitStack() as ctx:
        def sb(name, shape, dt=F32):
            return ctx.enter_context(nc.sbuf_tensor("p_" + name, shape, dt))

        def ps(name):
            return ctx.enter_context(nc.psum_tensor("p_bank_" + name, [P, 512], F32))

        def sem(name):
            return ctx.enter_context(nc.semaphore("p_s_" + name))

        ident = sb("ident", [P, P])
        wq, wk, wv = sb("wq", [P, P]), sb("wk", [P, P]), sb("wv", [P, P])
        qk_bias = sb("qk_bias", [P, 4])
        bias_q = sb("bias_q", [P, 1])
        bias_kl = sb("bias_kl", [P, 1])
        rel = sb("rel", [P, H, FAR + 1])
        relx = sb("relx", [P, H, FAR])
        bo = sb("bo", [P, E])
        X = [sb(f"x{s}", [P, NT, E]) for s in range(2)]
        XN = [sb(f"xn{s}", [P, NT, E]) for s in range(2)]
        Y = [sb(f"y{s}", [P, NT, E]) for s in range(2)]
        stats = sb("stats", [P, NT, 6])
        mv = sb("mv", [P, NT, 2])
        pows = sb("pows", [P, 2])
        rstd = sb("rstd", [P, NT])
        ones = sb("ones", [P, H, 1])
        XNT = [sb(f"xnt{s}", [P, S]) for s in range(2)]
        T = [[sb(f"t{n}{s}", [P, S]) for s in range(2)] for n in range(3)]
        V = [sb(f"v{s}", [P, NT, E]) for s in range(2)]
        SP = [[[sb(f"sp{n}{c}{s}", [P, S], BF16) for s in range(2)] for c in range(PARTS)] for n in range(3)]
        rest = [sb(f"rest{n}", [P, S]) for n in range(3)]
        QR = [sb(f"qr{s}", [P, H, EXT]) for s in range(2)]
        b_xt, b_q, b_k, b_v = ps("xt"), ps("q"), ps("k"), ps("v")
        b_qr = [ps(f"qr{n}") for n in range(4)]

        const_in, x_in = sem("const_in"), [sem(f"x_in{s}") for s in range(2)]
        const_ok = sem("const_ok")
        dve = sem("dve")
        pool = sem("pool")
        xn_ok, xnt_ps, xnt_ok = sem("xn_ok"), sem("xnt_ps"), sem("xnt_ok")
        q_ps, k_ps, v_ps = sem("q_ps"), sem("k_ps"), sem("v_ps")
        q_ok, k_ok, kl_ok, v_ok = sem("q_ok"), sem("k_ok"), sem("kl_ok"), sem("v_ok")
        qr_ps, qr_ev, qr_ok = sem("qr_ps"), sem("qr_ev"), sem("qr_ok")
        y_ok = sem("y_ok")
        mv_ok, rstd_ok = sem("mv_ok"), sem("rstd_ok")
        stats_ok = sem("stats_ok")
        sp_ok = [sem(f"sp_ok{n}") for n in range(3)]
        out_x, out_v = [sem(f"out_x{s}") for s in range(2)], [sem(f"out_v{s}") for s in range(2)]
        out_sp, out_qr = [sem(f"out_sp{s}") for s in range(2)], [sem(f"out_qr{s}") for s in range(2)]

        HALFN = H // 2 * FAR
        NSP = 16 * 3 * SLOTS
        block = ctx.enter_context(nc.Block())

        @block.sync
        def _(sp):
            for dst, src in ((ident, ident_dram), (wq, w["wq"]), (wk, w["wk"]), (wv, w["wv"]),
                             (qk_bias, w["qk_bias"]), (rel, w["rel"])):
                sp.dma_start(dst[:], src).then_inc(const_in, 16)
            sp.dma_start(bo[:], w["bo"].partition_broadcast(P)).then_inc(const_in, 16)
            with sp.Fori(0, B // 2) as i:
                for s in range(2):
                    sp.wait_ge(y_ok, i * 2 + s + 1)
                    sp.wait_ge(xn_ok, i * 2 + s + 1)
                    sp.dma_start(X[s][:], x[i * 2 + s].rearrange("(t p) e -> p t e", p=P)).then_inc(x_in[s], 16)
                for s in range(2):
                    b = i * 2 + s
                    sp.wait_ge(y_ok, b + 3)
                    sp.dma_start(scr["y"][b], Y[s][:]).then_inc(out_x[s], 16)
                    sp.wait_ge(xn_ok, b + 3)
                    sp.dma_start(scr["xn"][b], XN[s][:]).then_inc(out_x[s], 16)
                    sp.wait_ge(v_ok, b + 3)
                    sp.dma_start(scr["v"][b], V[s][:]).then_inc(out_v[s], 16)
                    for n in range(3):
                        sp.wait_ge(sp_ok[n], b + 3)
                        for slot in range(SLOTS):
                            part = (Q_PART if n == 0 else K_PART)[slot]
                            sp.dma_start(scr["stack"][b, n, :, slot], SP[n][part][s][:]).then_inc(out_sp[s], 16)
                    for t in range(NT):
                        sp.wait_ge(qr_ok, (b * NT + t) + 3)
                        sp.dma_start(scr["qr"][b, t], QR[t % 2][:]).then_inc(out_qr[t % 2], 16)
            for s in range(2):
                sp.wait_ge(out_x[s], 32 * B // 2 + 32)
                sp.wait_ge(out_v[s], 16 * B // 2 + 16)
                sp.wait_ge(out_sp[s], NSP * B // 2 + NSP)
                sp.wait_ge(out_qr[s], 16 * B * NT // 2 + 16)

        @block.vector
        def _(v):
            n = [0]

            def chain(ins):
                ins.then_inc(dve, 1)
                n[0] += 1

            v.wait_ge(const_in, 16 * 7)
            nc.vector.tensor_scalar(bias_q[:], qk_bias[:, 0:1], Q_SCALE, None, ALU.mult).then_inc(const_ok, 1)
            chain(nc.vector.tensor_tensor(bias_kl[:], qk_bias[:, 2:3], qk_bias[:, 3:4], ALU.subtract))
            v.wait_ge(dve, 1)
            nc.vector.tensor_tensor(bias_kl[:], bias_kl[:], qk_bias[:, 1:2], ALU.add).then_inc(const_ok, 1)
            nc.vector.tensor_tensor(relx[:], rel[:, :, 0:FAR], rel[:, :, FAR:FAR + 1].to_broadcast([P, H, FAR]),
                                    ALU.subtract).then_inc(const_ok, 1)
            for s in range(2):
                nc.vector.memset(QR[s][:], 0.0).then_inc(const_ok, 1)
            nc.vector.memset(pows[:, 0:1], LN_EPS).then_inc(const_ok, 1)
            nc.vector.memset(pows[:, 1:2], -0.5).then_inc(const_ok, 1)
            nc.vector.memset(ones[:], 1.0).then_inc(const_ok, 1)
            for sm, val in ((y_ok, 2), (xn_ok, 2), (v_ok, 2), (q_ok, 1), (k_ok, 1), (kl_ok, 1), (xnt_ok, 1),
                            (sp_ok[0], 2), (sp_ok[1], 2), (sp_ok[2], 2), (qr_ok, 2), (qr_ev, 4),
                            (xnt_ps, 1), (qr_ps, 1), (v_ps, 1)):
                v.sem_inc(sm, val)
            for s in range(2):
                v.sem_inc(out_x[s], 32)
                v.sem_inc(out_v[s], 16)
                v.sem_inc(out_sp[s], NSP)
                v.sem_inc(out_qr[s], 16)
            per_row = 4
            with v.Fori(0, B // 2) as i:
                for s in range(2):
                    b = i * 2 + s
                    at = b * per_row + 1
                    v.wait_ge(x_in[s], i * 16 + 16)
                    v.wait_ge(xn_ok, b + 2)
                    for t in range(NT):
                        ins = nc.vector.bn_stats(stats[:, t, :], X[s][:, t, :])
                    ins.then_inc(dve, 1)
                    v.wait_ge(dve, at + 1)
                    v.sem_inc(stats_ok, 1)
                    for t in range(NT):
                        ins = nc.vector.bn_aggr(mv[:, t, :], stats[:, t, :])
                    ins.then_inc(mv_ok, 1)
                    v.wait_ge(rstd_ok, b + 1)
                    v.wait_ge(out_x[s], i * 32 + 32)
                    v.wait_ge(y_ok, b + 1)
                    v.wait_ge(xnt_ps, b + 1)
                    for t in range(NT):
                        ins = nc.vector.tensor_scalar(XN[s][:, t, :], X[s][:, t, :], mv[:, t, 0:1], rstd[:, t:t + 1],
                                                      ALU.subtract, ALU.mult)
                    ins.then_inc(xn_ok, 1)
                    v.wait_ge(q_ps, b + 1)
                    v.wait_ge(qr_ps, b * NT + 1)
                    nc.vector.tensor_scalar(T[0][s][:], b_q[:], Q_SCALE, bias_q[:], ALU.mult, ALU.add).then_inc(q_ok, 1)
                    v.wait_ge(q_ok, b + 2)
                    v.wait_ge(out_sp[s], i * NSP + NSP)
                    nc.vector.tensor_copy(SP[0][0][s][:], T[0][s][:]).then_inc(dve, 1)
                    v.wait_ge(dve, at + 2)
                    v.wait_ge(sp_ok[0], b + 2)
                    nc.vector.tensor_tensor(rest[0][:], T[0][s][:], SP[0][0][s][:], ALU.subtract).then_inc(dve, 1)
                    v.wait_ge(dve, at + 3)
                    nc.vector.tensor_copy(SP[0][1][s][:], rest[0][:]).then_inc(dve, 1)
                    v.wait_ge(dve, at + 4)
                    nc.vector.tensor_tensor(SP[0][2][s][:], rest[0][:], SP[0][1][s][:], ALU.subtract).then_inc(sp_ok[0], 1)
                    for t in range(NT):
                        k = b * NT + t
                        v.wait_ge(qr_ps, k + 2)
                        v.wait_ge(out_qr[t % 2], (i * 4 + s * 2 + t // 2) * 16 + 16)
                        for hf in range(2):
                            ins = nc.vector.tensor_copy(
                                QR[t % 2][:, hf * G:(hf + 1) * G, QBLK - 1:QBLK - 1 + FAR],
                                b_qr[2 * (t % 2) + hf][:, 0:HALFN].rearrange("p (h r) -> p h r", r=FAR))
                        ins.then_inc(qr_ev, 1)

        @block.gpsimd
        def _(g):
            per_row = 7
            g.wait_ge(const_ok, 8)
            with g.Fori(0, B // 2) as i:
                for s in range(2):
                    b = i * 2 + s
                    at = b * per_row
                    g.wait_ge(xn_ok, b + 2)
                    g.wait_ge(mv_ok, b + 1)
                    nc.gpsimd.tensor_tensor(rstd[:], mv[:, :, 1], pows[:, 0:1].to_broadcast([P, NT]), ALU.add).then_inc(pool, 1)
                    g.wait_ge(pool, at + 1)
                    nc.gpsimd.tensor_tensor(rstd[:], rstd[:], pows[:, 1:2].to_broadcast([P, NT]), ALU.pow).then_inc(rstd_ok, 1)
                    g.wait_ge(x_in[s], i * 16 + 16)
                    g.wait_ge(out_x[s], i * 32 + 32)
                    for t in range(NT):
                        ins = nc.gpsimd.tensor_tensor(Y[s][:, t, :], X[s][:, t, :], bo[:], ALU.add)
                    ins.then_inc(y_ok, 1)
                    g.wait_ge(out_sp[s], i * NSP + NSP)
                    a = at + 1
                    for n, ready in ((1, k_ok), (2, kl_ok)):
                        g.wait_ge(ready, b + 2)
                        nc.gpsimd.tensor_tensor(SP[n][0][s][:], T[n][s][:], ones[:, 0].to_broadcast([P, S]), ALU.mult
                                                ).then_inc(pool, 1)
                        a += 1
                        g.wait_ge(pool, a)
                        g.wait_ge(sp_ok[n], b + 2)
                        nc.gpsimd.tensor_tensor(rest[n][:], T[n][s][:], SP[n][0][s][:], ALU.subtract).then_inc(pool, 1)
                        a += 1
                        g.wait_ge(pool, a)
                        nc.gpsimd.tensor_tensor(SP[n][1][s][:], rest[n][:], ones[:, 0].to_broadcast([P, S]), ALU.mult
                                                ).then_inc(pool, 1)
                        a += 1
                        g.wait_ge(pool, a)
                        nc.gpsimd.tensor_tensor(SP[n][2][s][:], rest[n][:], SP[n][1][s][:], ALU.subtract).then_inc(sp_ok[n], 1)
                    for t in range(NT):
                        g.wait_ge(qr_ev, b * NT + t + 5)
                        nc.gpsimd.tensor_tensor(QR[t % 2][:, :, 0:QBLK - 1],
                                                QR[t % 2][:, :, QBLK - 1:QBLK].to_broadcast([P, H, QBLK - 1]),
                                                ones[:].to_broadcast([P, H, QBLK - 1]), ALU.mult).then_inc(qr_ok, 1)

        @block.scalar
        def _(act):
            act.wait_ge(const_in, 16 * 7)
            act.wait_ge(const_ok, 8)
            with act.Fori(0, B // 2) as i:
                for s in range(2):
                    b = i * 2 + s
                    act.wait_ge(xnt_ps, b + 2)
                    act.wait_ge(v_ps, b + 1)
                    nc.scalar.activation(XNT[s][:], b_xt[:], ACT.Copy).then_inc(xnt_ok, 1)
                    act.wait_ge(k_ps, b + 1)
                    act.wait_ge(sp_ok[1], b + 1)
                    nc.scalar.activation(T[1][s][:], b_k[:], ACT.Identity, bias=qk_bias[:, 1:2]).then_inc(k_ok, 1)
                    act.wait_ge(sp_ok[2], b + 1)
                    nc.scalar.activation(T[2][s][:], b_k[:], ACT.Identity, bias=bias_kl[:]).then_inc(kl_ok, 1)
                    act.wait_ge(v_ps, b + 2)
                    act.wait_ge(out_v[s], i * 16 + 16)
                    nc.scalar.activation(V[s][:], b_v[:].rearrange("p (t e) -> p t e", e=E), ACT.Copy).then_inc(v_ok, 1)

        @block.tensor
        def _(pe):
            pe.wait_ge(const_in, 16 * 7)
            pe.wait_ge(const_ok, 8)
            with pe.Fori(0, B // 2) as i:
                for s in range(2):
                    b = i * 2 + s
                    pe.wait_ge(xn_ok, b + 3)
                    pe.wait_ge(xnt_ok, b + 1)
                    for t in range(NT):
                        ins = nc.tensor.transpose(b_xt[:, t * P:(t + 1) * P], XN[s][:, t, :], ident[:])
                    ins.then_inc(xnt_ps, 1)
                    pe.wait_ge(xnt_ok, b + 2)
                    pe.wait_ge(q_ok, b + 1)
                    nc.tensor.matmul(b_q[:], wq[:], XNT[s][:], start=True, stop=True).then_inc(q_ps, 1)
                    pe.wait_ge(kl_ok, b + 1)
                    nc.tensor.matmul(b_k[:], wk[:], XNT[s][:], start=True, stop=True).then_inc(k_ps, 1)
                    pe.wait_ge(v_ok, b + 2)
                    for t in range(NT):
                        ins = nc.tensor.matmul(b_v[:, t * P:(t + 1) * P], XNT[s][:, t * P:(t + 1) * P], wv[:],
                                               start=True, stop=True)
                    ins.then_inc(v_ps, 1)
                    pe.wait_ge(q_ok, b + 2)
                    for t in range(NT):
                        pe.wait_ge(qr_ev, b * NT + t + 3)
                        for hf in range(2):
                            ins = nc.tensor.matmul(b_qr[2 * (t % 2) + hf][:, 0:HALFN], T[0][s][:, t * P:(t + 1) * P],
                                                   relx[:, hf * G:(hf + 1) * G, :], start=True, stop=True)
                        ins.then_inc(qr_ps, 1)


EDGES = (P,) + tuple(n * QBLK - MAX_REL for n in range(1, NQB + 1)) + (0,)
NE = len(EDGES)
NF = FAR
WIDE = P + FAR
MARGIN = 64
PROBS_AT = tuple(par * (MARGIN + P * H * WIDE) + MARGIN for par in range(2))
NJ = 4
UNITS = NT * H // NJ
FC = H * NF // P

JOBS = [(u, "probs", j) for u in range(UNITS) for j in range(NJ)]
JOBS += [(u, "features", n) for u in range(2, UNITS, 4) for n in range(2)] + [(7, "out", n) for n in range(2)]
JOBS.sort(key=lambda job: job[0])
OF_ROW_BEFORE = [(0, "probs", j) for j in range(NJ)] + [(2, "features", n) for n in range(2)]
OF_ROW_BEFORE += [(7, "out", n) for n in range(2)]


def jobs_before(b, job, bank=None):
    def count(jobs):
        return sum(bank is None or JOBS.index(x) % 2 == bank for x in jobs)

    earlier = JOBS[:JOBS.index(job)]
    if isinstance(b, int) and b == 0:
        return count([x for x in earlier if x not in OF_ROW_BEFORE])
    if isinstance(b, int) and b == B:
        return B * count(JOBS) - count(OF_ROW_BEFORE) + count([x for x in earlier if x in OF_ROW_BEFORE])
    return b * count(JOBS) - count(OF_ROW_BEFORE) + count(earlier)


def bank_of(job):
    return JOBS.index(job) % 2


def attend(nc, w, scr):
    with ExitStack() as ctx:
        def sb(name, shape, dt=F32):
            return ctx.enter_context(nc.sbuf_tensor("a_" + name, shape, dt))

        def ps(name, banks=1):
            return ctx.enter_context(nc.psum_tensor("a_bank_" + name, [P, banks, 512], F32))

        def sem(name):
            return ctx.enter_context(nc.semaphore("a_s_" + name))

        ident = sb("ident", [P, P])
        wo = sb("wo", [P, E])
        v_bias = sb("v_bias", [P, NE, E])
        feat_w = sb("feat_w", [P, FC, P])
        keep = sb("keep", [P, QBLK])
        Q, K, KL = ([sb(f"{n}{s}", [P, G, S], BF16) for s in range(2)] for n in ("q", "k", "kl"))
        v_in = sb("v_in", [P, NT, E])
        V = [sb(f"v{s}", [P, NE, NT, NJ, NJ * 32]) for s in range(2)]
        win = [sb(f"win{s}", [P, H, WIN]) for s in range(2)]
        probs = sb("probs", [P, NJ, S + 2 * MAX_REL])
        probs_t = [sb(f"probs_t{s}", [P, NJ, S]) for s in range(2)]
        neg_max = sb("neg_max", [P, NJ])
        sums = sb("sums", [P, NT, H])
        inv = sb("inv", [P, H, HD])
        left = sb("left", [P, H, QBLK])
        feat = sb("feat", [P, H, NF])
        feat_t = sb("feat_t", [P, FC - 1, P])
        last_t = sb("last_t", [P, NT, 2, P])
        att_t = sb("att_t", [P, NT, P])
        y_in = sb("y_in", [P, NT, E])
        o_sb = sb("o_sb", [P, NT, E])
        b_s = ps("s", NJ)
        b_pt = [ps(f"pt{n}") for n in range(2)]
        b_o, b_w = ps("o"), ps("w")

        const_in, const_ok, margin_out = sem("const_in"), sem("const_ok"), sem("margin_out")
        N_CONST_IN, N_CONST_OK = 16 * 7, 5
        qk_in, win_in = [sem(f"qk_in{s}") for s in range(2)], [sem(f"win_in{s}") for s in range(2)]
        v_in_ok, v_ok = sem("v_in_ok"), sem("v_ok")
        s_ps, max_ok, exp_ok = sem("s_ps"), sem("max_ok"), sem("exp_ok")
        pt_ps, pt_ev = sem("pt_ps"), [sem("pt_ev0"), sem("pt_ev1")]
        av_ps, w_ps, o_ev, w_ev = sem("av_ps"), sem("w_ps"), sem("o_ev"), sem("w_ev")
        p_out = [sem("p_out0"), sem("p_out1")]
        f_in, l_in, feat_ok = sem("f_in"), sem("l_in"), sem("feat_ok")
        inv_ok, att_ok = sem("inv_ok"), sem("att_ok")
        y_ld, y_ok, y_st = sem("y_ld"), sem("y_ok"), sem("y_st")
        pool = sem("pool")
        room, go = sem("room"), sem("go")

        def need(eng, sm, b, per_row, c):
            value = b * per_row + c
            if not (isinstance(value, int) and value <= 0):
                eng.wait_ge(sm, value)

        def job_done(eng, b, job):
            need(eng, pt_ps, jobs_before(b, job), 1, 1)

        def bank_free(eng, b, job):
            need(eng, pt_ev[bank_of(job)], jobs_before(b, job, bank_of(job)), 1, 0)

        def job_read(eng, b, job):
            need(eng, pt_ev[bank_of(job)], jobs_before(b, job, bank_of(job)), 1, 1)

        def rows(engine, row):
            row(0, 0, 0, first=True)
            with engine.Fori(0, B // 2 - 1) as i:
                row(i * 2 + 1, 1, i)
                row(i * 2 + 2, 0, i + 1)
            row(B - 1, 1, B // 2 - 1)
            row(B, 0, B // 2, tail=True)

        block = ctx.enter_context(nc.Block())

        @block.sync
        def _(sp):
            flat = win[0][:].rearrange("p h c -> p (h c)")
            for dst, src in ((ident[:], w["ident"]), (wo[:], w["wo"]), (v_bias[:], w["v_edges"]),
                             (feat_w[:], w["feat_w"]), (keep[:], w["keep"]),
                             (flat[:, 0:FC * P].rearrange("p (c e) -> p c e", e=P), w["feat_last"]),
                             (v_in[:, 0, :], w["bv"].partition_broadcast(P))):
                sp.dma_start(dst, src).then_inc(const_in, 16)

            def load_row(b, s):
                need(sp, s_ps, b, 2 * UNITS, -2 * UNITS)
                for n, dst in enumerate((Q, K, KL)):
                    for par in range(2):
                        sp.dma_start(dst[s][par * HALF:par * HALF + ROWS],
                                     scr["stack"][b, n, par].rearrange("s (d g) q -> (s d) g q", g=G)
                                     ).then_inc(qk_in[s], 16)

            def load_v(b):
                need(sp, v_ok, b, 1, 0)
                sp.dma_start(v_in[:], scr["v"][b]).then_inc(v_in_ok, 16)

            def load_win(b, t):
                for n in range(NQB):
                    own = scr["qr"][b, t, n * QBLK:(n + 1) * QBLK, :, QBLK - 1:QBLK - 1 + WIN]
                    (stride, count), *inner = own.ap
                    own = bass.AP(own.tensor, own.offset, [[stride - 1, count], *inner])
                    sp.dma_start(win[t % 2][n * QBLK:(n + 1) * QBLK], own).then_inc(win_in[t % 2], 16)

            def row(b, s, m, first=False, tail=False):
                last = isinstance(b, int) and b == B - 1
                for u in range(10 if tail else UNITS):
                    t = u // 4
                    if not tail and u % 4 == 0 and not (last and t == NT - 1):
                        need(sp, s_ps, b, 2 * UNITS, 8 * t)
                        load_win(b + (t == NT - 1), (t + 1) % NT)
                    if not tail and not last and u == 1:
                        load_row(b + 1, 1 - s)
                    if not tail and not last and u == 2:
                        load_v(b + 1)
                    if not first and u == 3:
                        need(sp, y_st, b, 16, 0)
                        sp.dma_start(y_in[:], scr["y"][b - 1]).then_inc(y_ld, 16)
                    if not first and u == 9:
                        sp.wait_ge(y_ok, b * 2 + 2)
                        sp.dma_start(scr["y"][b - 1], y_in[:]).then_inc(y_st, 16)
                    if tail:
                        continue
                    for pair in range(2):
                        if u % 4 == 0 and pair == 0:
                            need(sp, f_in, b, 16 * NT, 16 * (t - 1))
                            need(sp, l_in, b, 16 * NT, 16 * (t - 1))
                            sp.sem_inc(room, 1)
                        sp.wait_ge(exp_ok, b * 4 * UNITS + 4 * u + 2 * pair + 2)
                        at = PROBS_AT[t % 2] + (4 * 2 * pair + u % 4) * WIDE
                        sp.dma_start(bass.AP(scr["probs"].tensor, at, [[H * WIDE, P], [4 * WIDE, 2], [1, WIDE]]),
                                     probs[:, 2 * pair:2 * pair + 2, t * P:t * P + WIDE]).then_inc(p_out[pair], 16)
                    if u % 4 == 3:
                        for pair in range(2):
                            sp.wait_ge(p_out[pair], b * 16 * UNITS + 16 * (u + 1))
                        sp.sem_inc(room, 1)
                        if not (first and t == 0):
                            job_done(sp, b, (4 * t + 2, "features", 1))
                        sp.dma_start(feat[:, :, 1:], bass.AP(scr["probs"].tensor, PROBS_AT[t % 2] + 1,
                                                            [[H * WIDE + 1, P], [WIDE, H], [1, NF - 1]])
                                     ).then_inc(f_in, 16)
                        need(sp, feat_ok, b, NT, t)
                        sp.dma_start(left[:], bass.AP(scr["probs"].tensor, PROBS_AT[t % 2] - QBLK + 1,
                                                     [[H * WIDE + 1, P], [WIDE, H], [1, QBLK]])
                                     ).then_inc(l_in, 16)

            for sm, start in ((y_st, 16), (y_ok, 2)):
                sp.sem_inc(sm, start)
            sp.wait_ge(const_ok, N_CONST_OK)
            for at in PROBS_AT:
                sp.dma_start(bass.AP(scr["probs"].tensor, at - MARGIN, [[MARGIN, 1], [1, MARGIN]]),
                             probs[0:1, 0, 0:MARGIN]).then_inc(margin_out, 16)
            load_row(0, 0)
            load_v(0)
            load_win(0, 0)
            sp.wait_ge(margin_out, 32)
            rows(sp, row)
            sp.wait_ge(y_st, 16 * B + 16)

        @block.tensor
        def _(pe):
            pe.wait_ge(const_ok, N_CONST_OK)

            def scores(b, u, j, s):
                h, t = 4 * j + u % 4, u // 4
                need(pe, exp_ok, b, 4 * UNITS, 4 * (u - 1) + j + 1)
                pe.sem_inc(go, 1)
                par = slice((h % 2) * HALF, (h % 2) * HALF + ROWS)
                for keys, left_part in ((KL, True), (K, False)):
                    for n in range(NQB):
                        edge = t * P + n * QBLK - MAX_REL
                        cols = slice(0, edge) if left_part else slice(max(edge, 0), S)
                        if left_part and edge <= 0:
                            continue
                        at = t * P + n * QBLK
                        nc.tensor.matmul(b_s[n * QBLK:(n + 1) * QBLK, j, cols], Q[s][par, h // 2, at:at + QBLK],
                                         keys[s][par, h // 2, cols], start=left_part or edge <= 0, stop=False,
                                         skip_group_check=True)
                for n in range(NQB):
                    edge = t * P + n * QBLK - MAX_REL
                    lo, hi = max(edge, 0), min(edge + WIN, S)
                    ins = nc.tensor.matmul(b_s[n * QBLK:(n + 1) * QBLK, j, lo:hi], ident[:, n * QBLK:(n + 1) * QBLK],
                                           win[t % 2][:, h, lo - edge:hi - edge], start=False, stop=True,
                                           skip_group_check=True)
                if j % 2:
                    ins.then_inc(s_ps, 1)

            def transpose(b, u, j):
                job = (u, "probs", j)
                bank_free(pe, b, job)
                pe.wait_ge(exp_ok, b * 4 * UNITS + 4 * (u - 1) + j + 1)
                for t in range(NT):
                    ins = nc.tensor.transpose(b_pt[bank_of(job)][:, 0, t * P:(t + 1) * P],
                                              probs[:, j, MAX_REL + t * P:MAX_REL + (t + 1) * P], ident[:])
                ins.then_inc(pt_ps, 1)

            def attended(b, u, s):
                t, hh = u // 4, u % 4
                after = (b, u + 1) if u < UNITS - 1 else (b + 1, 0)
                for j in (2, 3):
                    job_read(pe, after[0], (after[1], "probs", j))
                if u == 0:
                    pe.wait_ge(v_ok, b + 1)
                    need(pe, o_ev, b, 1, 0)
                first = hh == 0
                for kt in range(NT):
                    if kt == t:
                        parts = [(n * QBLK, (n + 1) * QBLK, EDGES.index(max(n * QBLK - MAX_REL, 0)))
                                 for n in range(NQB)]
                    elif kt == t - 1:
                        parts = [(0, QBLK, EDGES.index(P - MAX_REL)), (QBLK, P, EDGES.index(P))]
                    else:
                        parts = [(0, P, EDGES.index(P if kt < t else 0))]
                    for lo, hi, edge in parts:
                        for j in range(NJ):
                            ins = nc.tensor.matmul(b_o[32 * j:32 * j + 32, 0, t * P + lo:t * P + hi],
                                                   V[s][:, edge, kt, j, hh * 32:hh * 32 + 32],
                                                   probs_t[u % 2][:, j, kt * P + lo:kt * P + hi],
                                                   start=first, stop=False, skip_group_check=True)
                        first = False
                ins.then_inc(av_ps, 1)

            def features(b, u):
                job, nxt = (u, "features", 0), (u, "features", 1)
                flat = feat[:].rearrange("p h f -> p (h f)")
                pe.wait_ge(feat_ok, b * NT + (u - 2) // 4)
                bank_free(pe, b, job)
                for c in range(FC - 1):
                    ins = nc.tensor.transpose(b_pt[bank_of(job)][:, 0, c * P:(c + 1) * P],
                                              flat[:, c * P:(c + 1) * P], ident[:])
                ins.then_inc(pt_ps, 1)
                pe.wait_ge(inv_ok, b * NT + (u - 2) // 4)
                bank_free(pe, b, nxt)
                nc.tensor.transpose(b_pt[bank_of(nxt)][:, 0, 0:P], flat[:, (FC - 1) * P:], ident[:])
                nc.tensor.transpose(b_pt[bank_of(nxt)][:, 0, P:2 * P], inv[:].rearrange("p h d -> p (h d)"),
                                    ident[:]).then_inc(pt_ps, 1)

            def weigh(b, u):
                t = ((u - 3) // 4 - 1) % NT
                for n in range(2):
                    job_read(pe, b, (u - 1, "features", n))
                if t == 0:
                    need(pe, w_ev, b, 1, 0)
                for c in range(FC):
                    ins = nc.tensor.matmul(b_w[:, 0, t * P:(t + 1) * P], feat_w[:, c, :],
                                           feat_t[:, c, :] if c < FC - 1 else last_t[:, t, 0, :],
                                           start=c == 0, stop=c == FC - 1)
                ins.then_inc(w_ps, 1)

            def project(b):
                pe.wait_ge(att_ok, b)
                for n in range(2):
                    job = (7, "out", n)
                    bank_free(pe, b, job)
                    for t in (2 * n, 2 * n + 1):
                        ins = nc.tensor.matmul(b_pt[bank_of(job)][:, 0, (t % 2) * P:(t % 2 + 1) * P],
                                               att_t[:, t, :], wo[:], start=True, stop=True)
                    ins.then_inc(pt_ps, 1)

            def row(b, s, m, first=False, tail=False):
                for u in range(8 if tail else UNITS):
                    if u == 0 and not tail:
                        pe.wait_ge(qk_in[s], m * 96 + 96)
                    if u % 4 == 0 and not tail:
                        pe.wait_ge(win_in[u // 4 % 2], b * 128 + 64 * (u // 8 + 1))
                    for pair in ((0, 1), (2, 3)):
                        for j in pair:
                            if not tail:
                                scores(b, u, j, s)
                        for j in pair:
                            if (u and not tail) or (u == 0 and not first):
                                transpose(b, u, j)
                    if u > 1 and not tail:
                        attended(b, u - 2, s)
                    elif u < 2 and not first:
                        attended(b - 1, u + UNITS - 2, 1 - s)
                    if u % 4 == 2 and not (first if u == 2 else tail):
                        features(b, u)
                    if u % 4 == 3 and not (first if u == 3 else tail):
                        weigh(b, u)
                    if u == 7 and not first:
                        project(b)

            rows(pe, row)

        @block.vector
        def _(v):
            flat = win[0][:].rearrange("p h c -> p (h c)")
            nc.vector.memset(V[0][:], 0.0).then_inc(const_ok, 1)
            nc.vector.memset(probs[:], 0.0).then_inc(const_ok, 1)
            v.wait_ge(const_in, N_CONST_IN)
            nc.vector.tensor_tensor(v_bias[:], v_bias[:], v_in[:, 0:1, :].to_broadcast([P, NE, E]),
                                    ALU.add).then_inc(const_ok, 1)
            nc.vector.tensor_tensor(feat_w[:], feat_w[:], flat[:, 0:FC * P].rearrange("p (c e) -> p c e", e=P),
                                    ALU.subtract).then_inc(const_ok, 1)

            def read_probs(b, u, j):
                job = (u, "probs", j)
                job_done(v, b, job)
                need(v, av_ps, b, UNITS, u - 2)
                nc.vector.tensor_copy(probs_t[(u - 1) % 2][:, j, :], b_pt[bank_of(job)][:, 0, :]
                                      ).then_inc(pt_ev[bank_of(job)], 1)

            def row(b, s, m, first=False, tail=False):
                for u in range(8 if tail else UNITS):
                    for pair in range(2):
                        if not tail:
                            v.wait_ge(s_ps, b * 2 * UNITS + 2 * u + pair + 1)
                            need(v, exp_ok, b, 4 * UNITS, 4 * (u - 1) + 2 * pair + 2)
                            nc.vector.tensor_reduce(neg_max[:, 2 * pair:2 * pair + 2], b_s[:, 2 * pair:2 * pair + 2, :],
                                                    AX.X, ALU.max, negate=True).then_inc(max_ok, 1)
                        if (u and not tail) or (u == 0 and not first):
                            read_probs(b, u, 2 * pair + 1)
                    if u % 4 == 1 and not (first if u == 1 else tail):
                        t = (u // 4 - 1) % NT
                        need(v, exp_ok, b, 4 * UNITS, 4 * (u - 1))
                        if not (isinstance(b, int) and b == 0 and u == 5):
                            job_done(v, b if u > 1 else b - 1, ((u - 3) % UNITS, "features", 1))
                        nc.vector.reciprocal(inv[:], sums[:, t, :].rearrange("p (h o) -> p h o", o=1)
                                             .to_broadcast([P, H, HD])).then_inc(inv_ok, 1)
                    if u % 4 == 2 and not (first if u == 2 else tail):
                        job = (u, "features", 1)
                        t = (u // 4 - 1) % NT
                        job_done(v, b, job)
                        if t == 0:
                            need(v, att_ok, b, 1, 0)
                        nc.vector.tensor_copy(last_t[:, t].rearrange("p a q -> p (a q)"),
                                              b_pt[bank_of(job)][:, 0, 0:2 * P]).then_inc(pt_ev[bank_of(job)], 1)
                    if u == 4 and not first:
                        v.wait_ge(w_ps, b * NT)
                        v.wait_ge(o_ev, b)
                        if not (isinstance(b, int) and b == 1):
                            job_done(v, b - 1, (7, "out", 1))
                        nc.vector.tensor_tensor(att_t[:], o_sb[:], b_w[:, 0, :].rearrange("p (t q) -> p t q", q=P),
                                                ALU.add).then_inc(w_ev, 1)
                        v.wait_ge(w_ev, b)
                        job_read(v, b, (2, "features", 1))
                        nc.vector.tensor_tensor(att_t[:], att_t[:], last_t[:, :, 1, :], ALU.mult).then_inc(att_ok, 1)
                    if u == 7 and not first:
                        job = (7, "out", 1)
                        job_done(v, b, job)
                        v.wait_ge(y_ld, b * 16)
                        nc.vector.tensor_tensor(y_in[:, 2:4, :], y_in[:, 2:4, :],
                                                b_pt[bank_of(job)][:, 0, 0:2 * P].rearrange("p (t e) -> p t e", e=E),
                                                ALU.add).then_inc(pt_ev[bank_of(job)], 1)
                        job_read(v, b, job)
                        v.sem_inc(y_ok, 1)

            rows(v, row)

        @block.scalar
        def _(act):
            act.wait_ge(const_ok, N_CONST_OK)

            def read_probs(b, u, j):
                job = (u, "probs", j)
                job_done(act, b, job)
                need(act, av_ps, b, UNITS, u - 2)
                nc.scalar.activation(probs_t[(u - 1) % 2][:, j, :], b_pt[bank_of(job)][:, 0, :], ACT.Copy
                                     ).then_inc(pt_ev[bank_of(job)], 1)

            def row(b, s, m, first=False, tail=False):
                for u in range(8 if tail else UNITS):
                    t = u // 4
                    for pair in range(2):
                        if (u and not tail) or (u == 0 and not first):
                            read_probs(b, u, 2 * pair)
                        if tail:
                            continue
                        act.wait_ge(max_ok, b * 2 * UNITS + 2 * u + pair + 1)
                        need(act, p_out[pair], b, 16 * UNITS, 16 * u)
                        if u % 4 == 0:
                            need(act, inv_ok, b, NT, t + 1 - NT)
                        for j in (2 * pair, 2 * pair + 1):
                            if u or not first:
                                job_done(act, b, (u, "probs", j))
                            h = 4 * j + u % 4
                            nc.scalar.activation(probs[:, j, MAX_REL:MAX_REL + S], b_s[:, j, :], ACT.Exp,
                                                 bias=neg_max[:, j:j + 1], accum_out=sums[:, t, h:h + 1]
                                                 ).then_inc(exp_ok, 1)
                    if u == 1 and not first:
                        act.wait_ge(av_ps, b * UNITS)
                        need(act, y_ok, b, 2, 0)
                        nc.scalar.activation(o_sb[:], b_o[:, 0, :].rearrange("p (t q) -> p t q", q=P), ACT.Copy
                                             ).then_inc(o_ev, 1)
                    if u % 4 == 2 and not (first if u == 2 else tail):
                        job = (u, "features", 0)
                        job_done(act, b, job)
                        need(act, w_ps, b, NT, u // 4 - 1)
                        nc.scalar.activation(feat_t[:], b_pt[bank_of(job)][:, 0, :].rearrange("p (c q) -> p c q", q=P),
                                             ACT.Copy).then_inc(pt_ev[bank_of(job)], 1)
                    if u == 7 and not first:
                        job = (7, "out", 0)
                        job_done(act, b, job)
                        act.wait_ge(w_ev, b)
                        nc.scalar.activation(o_sb[:, 0:2, :], b_pt[bank_of(job)][:, 0, 0:2 * P]
                                             .rearrange("p (t e) -> p t e", e=E), ACT.Copy
                                             ).then_inc(pt_ev[bank_of(job)], 1)

            rows(act, row)

        @block.gpsimd
        def _(g):
            nc.gpsimd.memset(V[1][:], 0.0).then_inc(const_ok, 1)
            g.wait_ge(const_ok, N_CONST_OK)

            def make_v(b, kt, s):
                if kt == 0:
                    g.wait_ge(v_in_ok, b * 16 + 16)
                    need(g, av_ps, b, UNITS, -UNITS)
                for e in range(NE):
                    one = V[s][:, e, kt]
                    part, (sj, nj) = one.ap[0], one.ap[1]
                    out = bass.AP(one.tensor, one.offset, [part, [sj, nj], [32 + HD, NJ], [1, HD]])
                    ins = nc.gpsimd.tensor_tensor(out, v_in[:, kt, :].rearrange("p (j h d) -> p j h d", j=NJ, d=HD),
                                                  v_bias[:, e, :].rearrange("p (j h d) -> p j h d", j=NJ, d=HD), ALU.add)
                if kt == NT - 1:
                    ins.then_inc(v_ok, 1)

            def make_feature(b, t):
                at = 5 * (b * NT + t)
                g.wait_ge(l_in, b * 16 * NT + 16 * (t + 1))
                nc.gpsimd.tensor_tensor(left[:], left[:], keep[:].rearrange("p (o c) -> p o c", o=1)
                                        .to_broadcast([P, H, QBLK]), ALU.mult).then_inc(pool, 1)
                n = QBLK // 2
                for k in range(4):
                    g.wait_ge(pool, at + k + 1)
                    nc.gpsimd.tensor_tensor(left[:, :, 0:n], left[:, :, 0:n], left[:, :, n:2 * n], ALU.add).then_inc(pool, 1)
                    n //= 2
                g.wait_ge(pool, at + 5)
                g.wait_ge(f_in, b * 16 * NT + 16 * (t + 1))
                nc.gpsimd.tensor_tensor(feat[:, :, 0:1], left[:, :, 0:1], left[:, :, 1:2], ALU.add).then_inc(feat_ok, 1)

            for kt in range(NT):
                make_v(0, kt, 0)

            def row(b, s, m, first=False, tail=False):
                last = isinstance(b, int) and b == B - 1
                if not first:
                    make_feature(b - 1, NT - 1)
                for t in range(NT - 1 if not tail else 0):
                    if not last:
                        make_v(b + 1, t, 1 - s)
                    if t == 1 and not first:
                        add_out(b)
                    make_feature(b, t)
                if not tail and not last:
                    make_v(b + 1, NT - 1, 1 - s)
                if tail:
                    add_out(b)

            def add_out(b):
                job_read(g, b, (7, "out", 0))
                g.wait_ge(y_ld, b * 16)
                nc.gpsimd.tensor_tensor(y_in[:, 0:2, :], y_in[:, 0:2, :], o_sb[:, 0:2, :], ALU.add).then_inc(y_ok, 1)

            rows(g, row)


H2, D2 = 4, 32
MIX_JOBS = [(u, "probs", j) for u in range(NT) for j in range(H2)]
MIX_OLD = [(0, "probs", j) for j in range(H2)] + [(1, "inv", 0), (3, "out", 0)]
MIX_NEW = [(1, "nx", 0), (2, "q", 0), (2, "k", 0), (3, "v", 0)]
for _new in ((1, "inv", 0), (1, "nx", 0), (2, "q", 0), (2, "k", 0), (3, "v", 0), (3, "out", 0)):
    MIX_JOBS.append(_new)
MIX_JOBS.sort(key=lambda job: job[0])


def mix_jobs_before(b, job, bank=None):
    def count(jobs):
        return sum(bank is None or MIX_JOBS.index(x) % 2 == bank for x in jobs)

    def of_row(n):
        return [x for x in MIX_JOBS if not (n in (-1, 0) and x in MIX_OLD or n in (B - 1, B) and x in MIX_NEW
                                            or n in (-1, B) and x not in MIX_OLD + MIX_NEW)]

    earlier = MIX_JOBS[:MIX_JOBS.index(job)]
    if isinstance(b, int):
        return sum(count(of_row(n)) for n in range(-1, b)) + count([x for x in earlier if x in of_row(b)])
    return b * count(MIX_JOBS) + count(of_row(-1)) - count(MIX_OLD) + count(earlier)


def mix(nc, w, scr):
    with ExitStack() as ctx:
        def sb(name, shape, dt=F32):
            return ctx.enter_context(nc.sbuf_tensor("m_" + name, shape, dt))

        def ps(name, banks=1):
            return ctx.enter_context(nc.psum_tensor("m_bank_" + name, [P, banks, 512], F32))

        def sem(name):
            return ctx.enter_context(nc.semaphore("m_s_" + name))

        ident, wq, wk, wo = (sb(n, [P, P]) for n in ("ident", "wq", "wk", "wo"))
        wv = sb("wv", [P, D2])
        g1 = sb("g1", [P, 1])
        pows = sb("pows", [P, 1])
        ones = sb("ones", [P, NT * H2 * D2])
        xn = sb("xn", [P, NT, E])
        nx = sb("nx", [P, NT, E])
        square = sb("square", [P, E])
        mean_sq = sb("mean_sq", [P, NT])
        rms = sb("rms", [P, NT])
        nx_t = sb("nx_t", [P, S])
        Q, K = ([sb(f"{n}{s}", [P, S]) for s in range(2)] for n in ("q", "k"))
        V = [sb(f"v{s}", [P, NT, D2]) for s in range(2)]
        probs = sb("probs", [P, H2, S])
        probs_t = [sb(f"probs_t{s}", [P, H2, S]) for s in range(2)]
        neg_max = sb("neg_max", [P, H2])
        sums = [sb(f"sums{s}", [P, NT, H2]) for s in range(2)]
        inv = sb("inv", [P, NT, H2])
        inv_wide = sb("inv_wide", [P, NT, H2, D2])
        inv_t = sb("inv_t", [P, S])
        att_t = sb("att_t", [P, NT, P])
        xo = sb("xo", [P, NT, E])
        b_s = ps("s", H2)
        b_pt = [ps(f"pt{n}") for n in range(2)]
        b_o = ps("o")

        const_in, const_ok = sem("const_in"), sem("const_ok")
        N_IN = 16 * 6
        xn_in, sq_ok, ms_ok, rms_ok, nx_ok = sem("xn_in"), sem("sq_ok"), sem("ms_ok"), sem("rms_ok"), sem("nx_ok")
        s_ps, max_ok, exp_ok = sem("s_ps"), sem("max_ok"), sem("exp_ok")
        pt_ps, pt_ev = sem("pt_ps"), [sem("pt_ev0"), sem("pt_ev1")]
        av_ps, inv_ok, wide_ok, att_ok = sem("av_ps"), sem("inv_ok"), sem("wide_ok"), sem("att_ok")
        xo_in, xo_out = sem("xo_in"), sem("xo_out")

        def need(eng, sm, b, per_row, c):
            value = b * per_row + c
            if not (isinstance(value, int) and value <= 0):
                eng.wait_ge(sm, value)

        def bank_of(job):
            return MIX_JOBS.index(job) % 2

        def job_done(eng, b, job):
            need(eng, pt_ps, mix_jobs_before(b, job), 1, 1)

        def bank_free(eng, b, job):
            need(eng, pt_ev[bank_of(job)], mix_jobs_before(b, job, bank_of(job)), 1, 0)

        def job_read(eng, b, job):
            need(eng, pt_ev[bank_of(job)], mix_jobs_before(b, job, bank_of(job)), 1, 1)

        def rows(engine, row):
            row(-1, 1, "lead")
            row(0, 0, "first")
            with engine.Fori(0, B // 2 - 1) as i:
                row(i * 2 + 1, 1, "")
                row(i * 2 + 2, 0, "")
            row(B - 1, 1, "last")
            row(B, 0, "tail")

        def parts(kind):
            return kind not in ("lead", "tail"), kind not in ("lead", "first"), kind not in ("last", "tail")

        block = ctx.enter_context(nc.Block())

        @block.sync
        def _(sp):
            for dst, src in ((ident[:], w["ident"]), (wq[:], w["m_wq"]), (wk[:], w["m_wk"]), (wo[:], w["m_wo"]),
                             (wv[:], w["m_wv"]), (g1[:], w["g1"])):
                sp.dma_start(dst, src).then_inc(const_in, 16)
            for sm, start in ((xo_out, 16), (wide_ok, 1), (inv_ok, 1), (att_ok, 1)):
                sp.sem_inc(sm, start)

            def row(b, s, kind):
                own, old, new = parts(kind)
                if new:
                    need(sp, nx_ok, b, 1, 1)
                    sp.dma_start(xn[:], scr["xn"][b + 1]).then_inc(xn_in, 16)
                if old:
                    need(sp, xo_out, b, 16, 0)
                    sp.dma_start(xo[:], scr["xn"][b - 1]).then_inc(xo_in, 16)
                    job_read(sp, b, (3, "out", 0))
                    sp.dma_start(scr["x1"][b - 1], xo[:]).then_inc(xo_out, 16)

            rows(sp, row)
            sp.wait_ge(xo_out, 16 * B + 16)

        @block.tensor
        def _(pe):
            pe.wait_ge(const_in, N_IN)

            def small(b, s, u, what):
                job = (u, what, 0)
                bank = b_pt[bank_of(job)]
                bank_free(pe, b, job)
                if what == "inv":
                    pe.wait_ge(wide_ok, b + 1)
                    for t in range(NT):
                        ins = nc.tensor.transpose(bank[:, 0, t * P:(t + 1) * P],
                                                  inv_wide[:, t].rearrange("p h d -> p (h d)"), ident[:])
                elif what == "nx":
                    need(pe, nx_ok, b, 1, 2)
                    for t in range(NT):
                        ins = nc.tensor.transpose(bank[:, 0, t * P:(t + 1) * P], nx[:, t, :], ident[:])
                elif what in ("q", "k"):
                    job_read(pe, b, (1, "nx", 0))
                    ins = nc.tensor.matmul(bank[:, 0, :], (wq if what == "q" else wk)[:], nx_t[:], start=True, stop=True)
                elif what == "v":
                    for t in range(NT):
                        ins = nc.tensor.matmul(bank[:, 0, t * D2:(t + 1) * D2], nx_t[:, t * P:(t + 1) * P], wv[:],
                                               start=True, stop=True)
                else:
                    pe.wait_ge(att_ok, b + 1)
                    for t in range(NT):
                        ins = nc.tensor.matmul(bank[:, 0, t * P:(t + 1) * P], att_t[:, t, :], wo[:], start=True, stop=True)
                ins.then_inc(pt_ps, 1)

            def attended(b, u, s):
                after = (b, u + 1) if u < NT - 1 else (b + 1, 0)
                for j in (2, 3):
                    job_read(pe, after[0], (after[1], "probs", j))
                if u == 0:
                    need(pe, att_ok, b, 1, 1)
                for kt in range(NT):
                    for h in range(H2):
                        ins = nc.tensor.matmul(b_o[32 * h:32 * h + 32, 0, u * P:(u + 1) * P], V[s][:, kt, :],
                                               probs_t[u % 2][:, h, kt * P:(kt + 1) * P],
                                               start=kt == 0, stop=kt == NT - 1, skip_group_check=True)
                ins.then_inc(av_ps, 1)

            def row(b, s, kind):
                own, old, new = parts(kind)
                for u in range(NT):
                    if u == 0 and own:
                        for job in ((2, "q", 0), (2, "k", 0), (3, "v", 0)):
                            job_read(pe, b - 1, job)
                    for pair in ((0, 1), (2, 3)):
                        if own:
                            for h in pair:
                                need(pe, exp_ok, b, 4 * NT, 4 * (u - 1) + h + 1)
                                ins = nc.tensor.matmul(b_s[:, h, :], Q[s][h * D2:(h + 1) * D2, u * P:(u + 1) * P],
                                                       K[s][h * D2:(h + 1) * D2, :], start=True, stop=True)
                            ins.then_inc(s_ps, 1)
                        if (own and u) or (old and not u):
                            for j in pair:
                                job = (u, "probs", j)
                                bank_free(pe, b, job)
                                pe.wait_ge(exp_ok, b * 4 * NT + 4 * (u - 1) + j + 1)
                                for t in range(NT):
                                    ins = nc.tensor.transpose(b_pt[bank_of(job)][:, 0, t * P:(t + 1) * P],
                                                              probs[:, j, t * P:(t + 1) * P], ident[:])
                                ins.then_inc(pt_ps, 1)
                    if u > 1 and own:
                        attended(b, u - 2, s)
                    elif u < 2 and old:
                        attended(b - 1, u + NT - 2, 1 - s)
                    for what, at, wanted in (("inv", 1, old), ("nx", 1, new), ("q", 2, new), ("k", 2, new),
                                             ("v", 3, new), ("out", 3, old)):
                        if at == u and wanted:
                            small(b, s, u, what)

            rows(pe, row)

        @block.vector
        def _(v):
            nc.vector.memset(pows[:], -0.5).then_inc(const_ok, 1)
            nc.vector.memset(ones[:], 1.0).then_inc(const_ok, 1)
            v.wait_ge(const_in, N_IN)

            def row(b, s, kind):
                own, old, new = parts(kind)
                for u in range(NT):
                    for pair in range(2):
                        if own:
                            v.wait_ge(s_ps, b * 2 * NT + 2 * u + pair + 1)
                            need(v, exp_ok, b, 4 * NT, 4 * (u - 1) + 2 * pair + 2)
                            nc.vector.tensor_reduce(neg_max[:, 2 * pair:2 * pair + 2], b_s[:, 2 * pair:2 * pair + 2, :],
                                                    AX.X, ALU.max, negate=True).then_inc(max_ok, 1)
                        if (own and u) or (old and not u):
                            job = (u, "probs", 2 * pair + 1)
                            job_done(v, b, job)
                            need(v, av_ps, b, NT, u - 2)
                            nc.vector.tensor_copy(probs_t[(u - 1) % 2][:, 2 * pair + 1, :], b_pt[bank_of(job)][:, 0, :]
                                                  ).then_inc(pt_ev[bank_of(job)], 1)
                    if u == 0 and old:
                        v.wait_ge(exp_ok, b * 4 * NT)
                        need(v, wide_ok, b, 1, 0)
                        nc.vector.reciprocal(inv[:], sums[1 - s][:]).then_inc(inv_ok, 1)
                    if u == 0 and new:
                        need(v, sq_ok, b, NT, 2 * NT)
                        need(v, rms_ok, b, 1, 1)
                        need(v, nx_ok, b, 1, 1)
                        nc.vector.tensor_scalar(rms[:], mean_sq[:], 1.0 / E, RMS_EPS, ALU.mult, ALU.add).then_inc(ms_ok, 1)
                        need(v, rms_ok, b, 1, 2)
                        if kind != "lead":
                            job_done(v, b - 1, (1, "nx", 0))
                        for t in range(NT):
                            ins = nc.vector.tensor_scalar(nx[:, t, :], xn[:, t, :], rms[:, t:t + 1], None, ALU.mult)
                        ins.then_inc(nx_ok, 1)
                    if u == 1 and new:
                        job = (1, "nx", 0)
                        job_done(v, b, job)
                        if kind != "lead":
                            job_done(v, b - 1, (3, "v", 0))
                        nc.vector.tensor_scalar(nx_t[:], b_pt[bank_of(job)][:, 0, :], g1[:], None, ALU.mult
                                                ).then_inc(pt_ev[bank_of(job)], 1)
                    if u == 2 and old:
                        job_read(v, b, (1, "inv", 0))
                        v.wait_ge(av_ps, b * NT)
                        if not (isinstance(b, int) and b == 1):
                            job_done(v, b - 1, (3, "out", 0))
                        nc.vector.tensor_tensor(att_t[:].rearrange("p t q -> p (t q)"), b_o[:, 0, :], inv_t[:], ALU.mult
                                                ).then_inc(att_ok, 1)
                    if u == 2 and new:
                        job = (2, "k", 0)
                        job_done(v, b, job)
                        need(v, s_ps, b, 2 * NT, 0)
                        nc.vector.tensor_copy(K[1 - s][:], b_pt[bank_of(job)][:, 0, :]).then_inc(pt_ev[bank_of(job)], 1)
                    if u == 3 and old:
                        job = (3, "out", 0)
                        job_done(v, b, job)
                        v.wait_ge(xo_in, b * 16)
                        nc.vector.tensor_tensor(xo[:], xo[:], b_pt[bank_of(job)][:, 0, :]
                                                .rearrange("p (t e) -> p t e", e=E), ALU.add
                                                ).then_inc(pt_ev[bank_of(job)], 1)

            rows(v, row)

        @block.gpsimd
        def _(g):
            g.wait_ge(const_ok, 2)

            def row(b, s, kind):
                own, old, new = parts(kind)
                if new:
                    need(g, ms_ok, b, 1, 2)
                    nc.gpsimd.tensor_tensor(rms[:], rms[:], pows[:].to_broadcast([P, NT]), ALU.pow).then_inc(rms_ok, 1)
                if old:
                    g.wait_ge(inv_ok, b + 1)
                    if not (isinstance(b, int) and b == 1):
                        job_done(g, b - 1, (1, "inv", 0))
                    nc.gpsimd.tensor_tensor(inv_wide[:], inv[:].rearrange("p t (h o) -> p t h o", o=1)
                                            .to_broadcast([P, NT, H2, D2]),
                                            ones[:].rearrange("p (t h d) -> p t h d", t=NT, h=H2), ALU.mult
                                            ).then_inc(wide_ok, 1)

            rows(g, row)

        @block.scalar
        def _(act):
            act.wait_ge(const_in, N_IN)

            def row(b, s, kind):
                own, old, new = parts(kind)
                if new:
                    need(act, xn_in, b, 16, 32)
                    need(act, ms_ok, b, 1, 1)
                    for t in range(NT):
                        need(act, sq_ok, b, NT, NT + t)
                        nc.scalar.activation(square[:], xn[:, t, :], ACT.Square, accum_out=mean_sq[:, t:t + 1]
                                             ).then_inc(sq_ok, 1)
                for u in range(NT):
                    for pair in range(2):
                        if (own and u) or (old and not u):
                            job = (u, "probs", 2 * pair)
                            job_done(act, b, job)
                            need(act, av_ps, b, NT, u - 2)
                            nc.scalar.activation(probs_t[(u - 1) % 2][:, 2 * pair, :], b_pt[bank_of(job)][:, 0, :],
                                                 ACT.Copy).then_inc(pt_ev[bank_of(job)], 1)
                        if not own:
                            continue
                        act.wait_ge(max_ok, b * 2 * NT + 2 * u + pair + 1)
                        if u == 0:
                            need(act, inv_ok, b, 1, 0)
                        for j in (2 * pair, 2 * pair + 1):
                            if u or old:
                                job_done(act, b, (u, "probs", j))
                            nc.scalar.activation(probs[:, j, :], b_s[:, j, :], ACT.Exp, bias=neg_max[:, j:j + 1],
                                                 accum_out=sums[s][:, u, j:j + 1]).then_inc(exp_ok, 1)
                    if u == 1 and old:
                        job = (1, "inv", 0)
                        job_done(act, b, job)
                        need(act, att_ok, b, 1, 0)
                        nc.scalar.activation(inv_t[:], b_pt[bank_of(job)][:, 0, :], ACT.Copy
                                             ).then_inc(pt_ev[bank_of(job)], 1)
                    if u == 2 and new:
                        job = (2, "q", 0)
                        job_done(act, b, job)
                        need(act, s_ps, b, 2 * NT, 0)
                        nc.scalar.activation(Q[1 - s][:], b_pt[bank_of(job)][:, 0, :], ACT.Copy, scale=D2 ** -0.5
                                             ).then_inc(pt_ev[bank_of(job)], 1)
                    if u == 3 and new:
                        job = (3, "v", 0)
                        job_done(act, b, job)
                        need(act, av_ps, b, NT, 0)
                        nc.scalar.activation(V[1 - s][:], b_pt[bank_of(job)][:, 0, 0:NT * D2]
                                             .rearrange("p (t d) -> p t d", d=D2), ACT.Copy
                                             ).then_inc(pt_ev[bank_of(job)], 1)

            rows(act, row)


NX = 8
FFN = [NX] + list(range(NX))
NEXP = NX + 1
TAKEN = -4.0


def experts(nc, w, scr, out):
    with ExitStack() as ctx:
        def sb(name, shape, dt=F32):
            return ctx.enter_context(nc.sbuf_tensor("e_" + name, shape, dt))

        def ps(name):
            return ctx.enter_context(nc.psum_tensor("e_bank_" + name, [P, 512], F32))

        def sem(name):
            return ctx.enter_context(nc.semaphore("e_s_" + name))

        ident = sb("ident", [P, P])
        w1, w3, w2 = (sb(n, [P, NEXP, P]) for n in ("w1", "w3", "w2"))
        wr = sb("wr", [P, NX])
        g2 = sb("g2", [P, 1])
        r_bias, rank = sb("r_bias", [P, NX]), sb("rank", [P, NX])
        minus_half, euler = sb("minus_half", [P, 1]), sb("euler", [P, 1])
        x1 = [sb(f"x1{s}", [P, NT, E]) for s in range(2)]
        y = [sb(f"y{s}", [P, NT, E]) for s in range(2)]
        nx = sb("nx", [P, NT, E])
        square = sb("square", [P, E])
        mean_sq, rms = sb("mean_sq", [P, NT]), sb("rms", [P, NT])
        nx_t = [sb(f"nx_t{s}", [P, S]) for s in range(2)]
        probs, eq, rest, one0, one1 = (sb("r_" + n, [P, NT, NX]) for n in ("probs", "eq", "rest", "one0", "one1"))
        top, total, top0, top1, key, w_0, w_1 = (sb("c_" + n, [P, NT]) for n in (
            "top", "total", "top0", "top1", "key", "w_0", "w_1"))
        comb = [sb(f"comb{s}", [P, NT, NX]) for s in range(2)]
        gate = [sb(f"gate{n}", [P, S]) for n in range(2)]
        hid = [sb(f"hid{n}", [P, S]) for n in range(2)]
        b_g, b_u, b_y = ([ps(f"{c}{n}") for n in range(2)] for c in "guy")
        b_t, b_r = ps("t"), ps("r")

        const_in, const_ok = sem("const_in"), sem("const_ok")
        N_IN = 16 * 8
        x_in, y_in, stored = sem("x_in"), sem("y_in"), sem("stored")
        sq_ok, ms_ok, rms_ok, nx_ok = sem("sq_ok"), sem("ms_ok"), sem("rms_ok"), sem("nx_ok")
        t_ps, t_ev, r_ps, r_ev, exp_in, exp_ok, comb_ok = (sem(n) for n in (
            "t_ps", "t_ev", "r_ps", "r_ev", "exp_in", "exp_ok", "comb_ok"))
        g_ps, u_ps, y_ps, gate_ok, hid_ok, y_ev, base_ok = (sem(n) for n in (
            "g_ps", "u_ps", "y_ps", "gate_ok", "hid_ok", "y_ev", "base_ok"))
        w_ok = sem("w_ok")
        routed = sem("routed")
        CHAIN = 18

        def need(eng, sm, b, per_row, c):
            value = b * per_row + c
            if not (isinstance(value, int) and value <= 0):
                eng.wait_ge(sm, value)

        def rows(engine, row):
            row(-1, 1, "lead")
            row(0, 0, "first")
            with engine.Fori(0, B // 2 - 1) as i:
                row(i * 2 + 1, 1, "")
                row(i * 2 + 2, 0, "")
            row(B - 1, 1, "last")

        def before(b, s, n):
            return (b, s, n - 1) if n else (b - 1, 1 - s, NEXP - 1)

        def buf(s, n):
            return (s * NEXP + n) % 2

        block = ctx.enter_context(nc.Block())

        @block.sync
        def _(sp):
            for dst, src in ((ident[:], w["ident"]), (w1[:], w["e_w1"]), (w3[:], w["e_w3"]), (w2[:], w["e_w2"]),
                             (wr[:], w["e_wr"]), (g2[:], w["g2"]), (r_bias[:], w["e_bias"].partition_broadcast(P)),
                             (rank[:], w["rank"].partition_broadcast(P))):
                sp.dma_start(dst, src).then_inc(const_in, 16)

            def store(b, s):
                sp.wait_ge(y_ev, b * NEXP + NEXP)
                sp.dma_start(out[b].rearrange("(t p) e -> p t e", p=P), y[s][:]).then_inc(stored, 16)

            def row(b, s, kind):
                if kind != "last":
                    need(sp, base_ok, b, 1, 1)
                    need(sp, nx_ok, b, 1, 1)
                    sp.dma_start(x1[1 - s][:], scr["x1"][b + 1]).then_inc(x_in, 16)
                if kind not in ("lead", "first"):
                    store(b - 1, 1 - s)
                    sp.wait_ge(stored, b * 16)
                if kind != "last":
                    sp.dma_start(y[1 - s][:], scr["y"][b + 1]).then_inc(y_in, 16)

            rows(sp, row)
            store(B - 1, 1)
            sp.wait_ge(stored, 16 * B)

        @block.tensor
        def _(pe):
            pe.wait_ge(const_in, N_IN)

            def up(b, s, n):
                e, k = FFN[n], buf(s, n)
                if n == 0:
                    need(pe, t_ev, b, 1, 1)
                need(pe, hid_ok, b, NEXP, n - 1)
                nc.tensor.matmul(b_g[k][:], w1[:, e, :], nx_t[s][:], start=True, stop=True).then_inc(g_ps, 1)
                nc.tensor.matmul(b_u[k][:], w3[:, e, :], nx_t[s][:], start=True, stop=True).then_inc(u_ps, 1)

            def down(b, s, n):
                e, k = FFN[n], buf(s, n)
                pe.wait_ge(hid_ok, b * NEXP + n + 1)
                need(pe, y_ev, b, NEXP, n - 1)
                for t in range(NT):
                    ins = nc.tensor.matmul(b_y[k][:, t * P:(t + 1) * P], hid[k][:, t * P:(t + 1) * P], w2[:, e, :],
                                           start=True, stop=True)
                ins.then_inc(y_ps, 1)

            def row(b, s, kind):
                for n in range(NEXP):
                    if kind != "lead":
                        up(b, s, n)
                        if n or kind != "first":
                            down(*before(b, s, n))
                    if n == 2 and kind != "last":
                        pe.wait_ge(nx_ok, b + 2)
                        need(pe, t_ev, b, 1, 1)
                        for t in range(NT):
                            ins = nc.tensor.transpose(b_t[:, t * P:(t + 1) * P], nx[:, t, :], ident[:])
                        ins.then_inc(t_ps, 1)
                    if n == 3 and kind != "last":
                        pe.wait_ge(t_ev, b + 2)
                        need(pe, r_ev, b, 1, 1)
                        for t in range(NT):
                            ins = nc.tensor.matmul(b_r[:, t * NX:(t + 1) * NX], nx_t[1 - s][:, t * P:(t + 1) * P], wr[:],
                                                   start=True, stop=True)
                        ins.then_inc(r_ps, 1)

            rows(pe, row)
            down(B - 1, 1, NEXP - 1)

        @block.scalar
        def _(act):
            act.wait_ge(const_in, N_IN)

            def row(b, s, kind):
                for n in range(NEXP):
                    if n == 1 and kind != "last":
                        need(act, x_in, b, 16, 32)
                        need(act, ms_ok, b, 1, 1)
                        for t in range(NT):
                            need(act, sq_ok, b, NT, NT + t)
                            nc.scalar.activation(square[:], x1[1 - s][:, t, :], ACT.Square,
                                                 accum_out=mean_sq[:, t:t + 1]).then_inc(sq_ok, 1)
                    if n == 3 and kind != "last":
                        need(act, t_ps, b, 1, 2)
                        need(act, u_ps, b, NEXP, 0)
                        need(act, r_ps, b, 1, 0)
                        nc.scalar.activation(nx_t[1 - s][:], b_t[:], ACT.Copy, scale=g2[:]).then_inc(t_ev, 1)
                    if kind != "lead":
                        act.wait_ge(g_ps, b * NEXP + n + 1)
                        need(act, hid_ok, b, NEXP, n - 1)
                        nc.scalar.activation(gate[buf(s, n)][:], b_g[buf(s, n)][:], ACT.Silu).then_inc(gate_ok, 1)

            rows(act, row)

        @block.vector
        def _(v):
            nc.vector.memset(minus_half[:], -0.5).then_inc(const_ok, 1)
            nc.vector.memset(euler[:], math.e).then_inc(const_ok, 1)
            v.wait_ge(const_in, N_IN)

            def add(b, s, n):
                k = buf(s, n)
                v.wait_ge(y_ps, b * NEXP + n + 1)
                if n == 0:
                    v.wait_ge(base_ok, b + 1)
                    nc.vector.tensor_tensor(y[s][:].rearrange("p t e -> p (t e)"), y[s][:].rearrange("p t e -> p (t e)"),
                                            b_y[k][:], ALU.add).then_inc(y_ev, 1)
                    return
                v.wait_ge(y_ev, b * NEXP + n)
                if n == 1:
                    v.wait_ge(comb_ok, b + 1)
                e = FFN[n]
                for t in range(NT):
                    ins = nc.vector.scalar_tensor_tensor(y[s][:, t, :], b_y[k][:, t * P:(t + 1) * P],
                                                         comb[s][:, t, e:e + 1], y[s][:, t, :], ALU.mult, ALU.add)
                ins.then_inc(y_ev, 1)

            def chain(b, k):
                need(v, routed, b, CHAIN, CHAIN + k)

            def each(col):
                return col[:].rearrange("p (t o) -> p t o", o=1).to_broadcast([P, NT, NX])

            def by_rank():
                return rank[:].rearrange("p (o e) -> p o e", o=1).to_broadcast([P, NT, NX])

            def pick(b, k, values, best, one):
                chain(b, k)
                nc.vector.tensor_reduce(best[:], values[:], AX.X, ALU.max).then_inc(routed, 1)
                chain(b, k + 1)
                nc.vector.tensor_tensor(eq[:], values[:], each(best), ALU.is_equal).then_inc(routed, 1)
                chain(b, k + 2)
                nc.vector.tensor_tensor(eq[:], eq[:], by_rank(), ALU.mult).then_inc(routed, 1)
                chain(b, k + 3)
                nc.vector.tensor_reduce(key[:], eq[:], AX.X, ALU.max).then_inc(routed, 1)
                chain(b, k + 4)
                nc.vector.tensor_tensor(one[:], eq[:], each(key), ALU.is_equal).then_inc(routed, 1)

            def logits(b):
                need(v, r_ps, b, 1, 2)
                need(v, comb_ok, b, 1, 1)
                nc.vector.tensor_tensor(probs[:], b_r[:, 0:NT * NX].rearrange("p (t e) -> p t e", e=NX),
                                        r_bias[:].rearrange("p (o e) -> p o e", o=1).to_broadcast([P, NT, NX]),
                                        ALU.add).then_inc(r_ev, 1)
                need(v, r_ev, b, 1, 2)
                nc.vector.tensor_reduce(top[:], probs[:], AX.X, ALU.max).then_inc(routed, 1)
                chain(b, 1)
                nc.vector.tensor_tensor(probs[:], probs[:], each(top), ALU.subtract).then_inc(exp_in, 1)

            def picks(b):
                need(v, exp_ok, b, 2, 3)
                nc.vector.tensor_reduce(total[:], probs[:], AX.X, ALU.add).then_inc(routed, 1)
                chain(b, 2)
                nc.vector.reciprocal(total[:], total[:]).then_inc(routed, 1)
                chain(b, 3)
                nc.vector.tensor_tensor(probs[:], probs[:], each(total), ALU.mult).then_inc(routed, 1)
                pick(b, 4, probs, top0, one0)
                chain(b, 9)
                nc.vector.scalar_tensor_tensor(rest[:], one0[:], TAKEN, probs[:], ALU.mult, ALU.add).then_inc(routed, 1)
                pick(b, 10, rest, top1, one1)
                chain(b, 15)
                nc.vector.tensor_tensor(w_1[:], top1[:], top0[:], ALU.subtract).then_inc(exp_in, 1)

            def weights(b, s):
                need(v, exp_ok, b, 2, 4)
                nc.vector.tensor_scalar(w_0[:], w_1[:], 1.0, None, ALU.add).then_inc(routed, 1)
                chain(b, 16)
                nc.vector.reciprocal(w_0[:], w_0[:]).then_inc(routed, 1)
                chain(b, 17)
                nc.vector.tensor_tensor(w_1[:], w_1[:], w_0[:], ALU.mult)
                nc.vector.tensor_tensor(one0[:], one0[:], each(w_0), ALU.mult).then_inc(routed, 1)
                chain(b, 18)
                nc.vector.tensor_tensor(one1[:], one1[:], each(w_1), ALU.mult).then_inc(w_ok, 1)
                need(v, w_ok, b, 1, 2)
                need(v, y_ev, b, NEXP, 0)
                nc.vector.tensor_tensor(comb[1 - s][:], one0[:], one1[:], ALU.add).then_inc(comb_ok, 1)

            def row(b, s, kind):
                for n in range(NEXP):
                    if kind != "lead":
                        q = b * NEXP + n + 1
                        v.wait_ge(gate_ok, q)
                        v.wait_ge(u_ps, q)
                        need(v, y_ps, b, NEXP, n - 1)
                        k = buf(s, n)
                        nc.vector.tensor_tensor(hid[k][:], gate[k][:], b_u[k][:], ALU.mult).then_inc(hid_ok, 1)
                        if n or kind != "first":
                            add(*before(b, s, n))
                    if kind == "last":
                        continue
                    if n == 1:
                        need(v, sq_ok, b, NT, 2 * NT)
                        need(v, nx_ok, b, 1, 1)
                        nc.vector.tensor_scalar(rms[:], mean_sq[:], 1.0 / E, RMS_EPS, ALU.mult, ALU.add).then_inc(ms_ok, 1)
                        need(v, rms_ok, b, 1, 2)
                        need(v, t_ps, b, 1, 1)
                        for t in range(NT):
                            ins = nc.vector.tensor_scalar(nx[:, t, :], x1[1 - s][:, t, :], rms[:, t:t + 1], None, ALU.mult)
                        ins.then_inc(nx_ok, 1)
                    if n == 4:
                        logits(b)
                    if n == 5:
                        picks(b)
                    if n == 6:
                        weights(b, s)

            rows(v, row)
            add(B - 1, 1, NEXP - 1)

        @block.gpsimd
        def _(g):
            g.wait_ge(const_ok, 2)

            def row(b, s, kind):
                if kind == "last":
                    return
                need(g, ms_ok, b, 1, 2)
                nc.gpsimd.tensor_tensor(rms[:], rms[:], minus_half[:].to_broadcast([P, NT]), ALU.pow).then_inc(rms_ok, 1)
                need(g, y_in, b, 16, 32)
                need(g, x_in, b, 16, 32)
                nc.gpsimd.tensor_tensor(y[1 - s][:], y[1 - s][:], x1[1 - s][:], ALU.add).then_inc(base_ok, 1)
                flat = probs[:].rearrange("p t e -> p (t e)")
                need(g, exp_in, b, 2, 3)
                nc.gpsimd.tensor_tensor(flat, euler[:].to_broadcast([P, NT * NX]), flat, ALU.pow).then_inc(exp_ok, 1)
                need(g, exp_in, b, 2, 4)
                nc.gpsimd.tensor_tensor(w_1[:], euler[:].to_broadcast([P, NT]), w_1[:], ALU.pow).then_inc(exp_ok, 1)

            rows(g, row)


def program(nc, a, out):
    scr = {
        "y": nc.dram_tensor("scr_y", (B, P, NT, E), F32, kind="Internal").ap(),
        "xn": nc.dram_tensor("scr_xn", (B, P, NT, E), F32, kind="Internal").ap(),
        "x1": nc.dram_tensor("scr_x1", (B, P, NT, E), F32, kind="Internal").ap(),
        "v": nc.dram_tensor("scr_v", (B, P, NT, E), F32, kind="Internal").ap(),
        "stack": nc.dram_tensor("scr_stack", (B, 3, 2, SLOTS, HALF, S), BF16, kind="Internal").ap(),
        "qr": nc.dram_tensor("scr_qr", (B, NT, P, H, EXT), F32, kind="Internal").ap(),
    }
    scr["probs"] = nc.dram_tensor("scr_probs", (2 * (MARGIN + P * H * WIDE),), F32, kind="Internal").ap()
    prepare(nc, a["x"], a, scr, a["ident"])
    attend(nc, a, scr)
    mix(nc, a, scr)
    experts(nc, a, scr, out)


def lay_out(inputs):
    import numpy as np

    g = {k: np.asarray(v) for k, v in inputs.items()}
    f = np.float32
    order = np.array([(2 * half + par) * HD + d for par in range(2) for d in range(HD) for half in range(G)])
    wide = np.array([d for par in range(2) for d in range(HD) for half in range(G)])
    rel_k, rel_v = g["L0_attn_rel_k"], g["L0_attn_rel_v"]
    rel = np.zeros((P, H, FAR + 1), f)
    for p in range(P):
        rel[p, order[p] // HD] = rel_k[:, wide[p]]
    key = np.arange(P)[:, None]
    v_edges = np.stack([np.where(key < edge, np.tile(rel_v[0], H), np.tile(rel_v[FAR], H)) for edge in EDGES], 1)
    feat_w, feat_last = np.zeros((P, FC, P), f), np.zeros((P, FC, P), f)
    for n in range(H * NF):
        h, r = divmod(n, NF)
        feat_w[n % P, n // P, h * HD:(h + 1) * HD] = rel_v[r]
        feat_last[n % P, n // P, h * HD:(h + 1) * HD] = rel_v[FAR]
    keep = (np.arange(QBLK)[None] - (QBLK - 1) >= -(key % QBLK)).astype(f)
    first = {n: np.concatenate([g["L0_ffn_e" + n], g["L0_ffn_s" + n][None]]).transpose(2, 0, 1)
             for n in ("W1", "W2", "W3")}
    return {
        "x": g["L0_attn_hidden_states"],
        "ident": np.eye(P, dtype=f),
        "wq": g["L0_attn_Wq"][order].T, "wk": g["L0_attn_Wk"][order].T, "wv": g["L0_attn_Wv"].T,
        "qk_bias": np.stack([g["L0_attn_bq"][order], g["L0_attn_bk"][order], rel_k[0][wide], rel_k[FAR][wide]], 1),
        "rel": rel,
        "bo": g["L0_attn_bo"],
        "wo": g["L0_attn_Wo"].T, "bv": g["L0_attn_bv"],
        "m_wq": g["L0_ffn_Wq"].T, "m_wk": np.tile(g["L0_ffn_Wkc"].T, (1, H2)), "m_wv": g["L0_ffn_Wvc"].T,
        "m_wo": g["L0_ffn_Wo"].T, "g1": g["L0_ffn_g1"][:, None], "g2": g["L0_ffn_g2"][:, None],
        "e_w1": first["W1"], "e_w3": first["W3"], "e_w2": first["W2"],
        "e_wr": g["L0_ffn_Wr"].T, "e_bias": g["L0_ffn_expert_bias"], "rank": np.arange(NX, 0, -1).astype(f),
        "v_edges": v_edges, "feat_w": feat_w, "feat_last": feat_last, "keep": keep,
    }


def kernel(**inputs):
    import numpy as np
    import concourse.bacc as bacc
    from concourse.bass_utils import run_bass_kernel_spmd

    nc = bacc.Bacc("TRN2", target_bir_lowering=False, num_devices=1)
    arrays = {"in_" + k: np.ascontiguousarray(v) for k, v in lay_out(inputs).items()}
    aps = {k[3:]: nc.dram_tensor(k, v.shape, mybir.dt.from_np(v.dtype), kind="ExternalInput").ap()
           for k, v in arrays.items()}
    out = nc.dram_tensor("out_0", (B, S, E), F32, kind="ExternalOutput").ap()
    program(nc, aps, out)
    return run_bass_kernel_spmd(nc, [arrays], core_ids=[0]).results[0]["out_0"]
```

```python
import math
from contextlib import ExitStack

import concourse.bass as bass
from concourse import mybir

F32 = mybir.dt.float32
BF16 = mybir.dt.bfloat16
ALU = mybir.AluOpType
ACT = mybir.ActivationFunctionType
AX = mybir.AxisListType

P = 128
B, S, E = 16, 512, 128
NT = S // P
H, HD = 16, 8
MAX_REL = 20
QBLK = 32
NQB = P // QBLK
FAR = 2 * MAX_REL
WIN = QBLK + FAR
SLOTS = 6
PARTS = 3
HALF = P // 2
ROWS = SLOTS * HD
G = H // 2
LN_EPS, RMS_EPS = 1e-5, 1e-6
Q_SCALE = HD ** -0.5
Q_PART = (0, 0, 0, 1, 1, 2)
K_PART = (0, 1, 2, 0, 1, 0)


def prepare(nc, x, w, scr, ident_dram):
    with ExitStack() as ctx:
        def sb(name, shape, dt=F32):
            return ctx.enter_context(nc.sbuf_tensor("p_" + name, shape, dt))

        def ps(name):
            return ctx.enter_context(nc.psum_tensor("p_bank_" + name, [P, 512], F32))

        def sem(name):
            return ctx.enter_context(nc.semaphore("p_s_" + name))

        ident = sb("ident", [P, P])
        wq, wk, wv = sb("wq", [P, P]), sb("wk", [P, P]), sb("wv", [P, P])
        qk_bias = sb("qk_bias", [P, 4])
        bias_q = sb("bias_q", [P, 1])
        bias_kl = sb("bias_kl", [P, 1])
        rel = sb("rel", [P, H, FAR + 1])
        relx = sb("relx", [P, H, FAR])
        bo = sb("bo", [P, E])
        X = [sb(f"x{s}", [P, NT, E]) for s in range(2)]
        XN = [sb(f"xn{s}", [P, NT, E]) for s in range(2)]
        Y = [sb(f"y{s}", [P, NT, E]) for s in range(2)]
        stats = sb("stats", [P, NT, 6])
        mv = sb("mv", [P, NT, 2])
        pows = sb("pows", [P, 2])
        ones = sb("ones", [P, H])
        rstd = sb("rstd", [P, NT])
        XNT = [sb(f"xnt{s}", [P, S]) for s in range(2)]
        T = [[sb(f"t{n}{s}", [P, S]) for s in range(2)] for n in range(3)]
        SP = [[[sb(f"sp{n}{c}{s}", [P, S], BF16) for s in range(2)] for c in range(PARTS)] for n in range(3)]
        rest = [sb(f"rest{n}", [P, S]) for n in range(3)]
        V = [sb(f"v{s}", [P, NT, E]) for s in range(2)]
        QR = [sb(f"qr{t}", [P, H, FAR]) for t in range(NT)]
        QR0 = [sb(f"qr0{s}", [P, NT, H]) for s in range(2)]
        b_xt, b_q, b_k, b_v = ps("xt"), ps("q"), ps("k"), ps("v")
        b_qr = [[ps(f"qr{n}{hf}") for hf in range(2)] for n in range(2)]

        const_in, const_ok, x_in = sem("const_in"), sem("const_ok"), [sem(f"x_in{s}") for s in range(2)]
        N_CONST = 8
        stats_ok, mv_ok, rstd_add, rstd_ok = sem("stats_ok"), sem("mv_ok"), sem("rstd_add"), sem("rstd_ok")
        stats_go = sem("stats_go")
        xn_ok, xnt_ps, xnt_ok, y_ok = sem("xn_ok"), sem("xnt_ps"), sem("xnt_ok"), sem("y_ok")
        q_ps, k_ps, v_ps = sem("q_ps"), sem("k_ps"), sem("v_ps")
        t_ok, hi_ok, rest_ok, mid_ok, lo_ok = ([sem(f"{n}{c}") for c in range(3)] for n in (
            "t_ok", "hi_ok", "rest_ok", "mid_ok", "lo_ok"))
        v_ok, qr_ps, qr_ev, qr0_ok = sem("v_ok"), sem("qr_ps"), [sem("qr_ev0"), sem("qr_ev1")], sem("qr0_ok")
        out_x, out_v, out_0 = ([sem(f"out_{n}{s}") for s in range(2)] for n in "xv0")
        out_sp, out_qr = [sem(f"out_sp{s}") for s in range(2)], [sem(f"out_qr{t}") for t in range(NT)]
        end_out = sem("end_out")

        def need(eng, sm, b, per_row, c):
            value = b * per_row + c
            if not (isinstance(value, int) and value <= 0):
                eng.wait_ge(sm, value)

        def rows(engine, row):
            row(-1, 1, -1)
            row(0, 0, 0)
            row(1, 1, 0)
            row(2, 0, 1)
            with engine.Fori(0, (B - 6) // 2) as i:
                row(i * 2 + 3, 1, i + 1)
                row(i * 2 + 4, 0, i + 2)
            for b in range(B - 3, B):
                row(b, b % 2, b // 2)

        def own(b):
            return not (isinstance(b, int) and b < 0)

        def new(b):
            return not (isinstance(b, int) and b == B - 1)

        block = ctx.enter_context(nc.Block())

        @block.sync
        def _(sp):
            def load_x(b, s):
                sp.dma_start(X[s][:], x[b].rearrange("(t p) e -> p t e", p=P)).then_inc(x_in[s], 16)

            load_x(0, 0)
            for dst, src in ((ident, ident_dram), (wq, w["wq"]), (wk, w["wk"]), (wv, w["wv"]),
                             (qk_bias, w["qk_bias"]), (rel, w["rel"])):
                sp.dma_start(dst[:], src).then_inc(const_in, 16)
            sp.dma_start(bo[:], w["bo"].partition_broadcast(P)).then_inc(const_in, 16)
            load_x(1, 1)
            sp.wait_ge(const_in, 16 * 7)
            sp.dma_start(scr["qr"][B * NT, 0:1, 0:1], ident[0:1, 0:1]).then_inc(end_out, 16)

            def row(b, s, m):
                if not own(b):
                    return
                need(sp, y_ok, b, 1, 1)
                sp.dma_start(scr["y"][b], Y[s][:]).then_inc(out_x[s], 16)
                need(sp, xn_ok, b, 1, 1)
                sp.dma_start(scr["xn"][b], XN[s][:]).then_inc(out_x[s], 16)
                if not (isinstance(b, int) and b + 2 >= B):
                    load_x(b + 2, s)
                def store_qr(t):
                    for hf in range(2):
                        need(sp, qr_ev[hf], b, NT, t + 1)
                    sp.dma_start(scr["qr"][b * NT + t], QR[t][:].rearrange("p h r -> p (h r)")).then_inc(out_qr[t], 16)

                for part, ready in ((0, hi_ok), (1, mid_ok), (2, lo_ok)):
                    for n in (0, 1, 2):
                        need(sp, ready[n], b, 1, 1)
                        sp.dma_start(scr["parts"][b, n, part], SP[n][part][s][:]).then_inc(out_sp[s], 16)
                    if part == 0:
                        need(sp, v_ok, b, 1, 1)
                        sp.dma_start(scr["v"][b], V[s][:]).then_inc(out_v[s], 16)
                    store_qr(part)
                store_qr(NT - 1)
                need(sp, qr0_ok, b, NT, NT)
                sp.dma_start(scr["qr0"][b], QR0[s][:]).then_inc(out_0[s], 16)

            rows(sp, row)
            sp.wait_ge(end_out, 16)
            for s in range(2):
                sp.wait_ge(out_x[s], 32 * B // 2)
                sp.wait_ge(out_v[s], 16 * B // 2)
                sp.wait_ge(out_0[s], 16 * B // 2)
                sp.wait_ge(out_sp[s], 16 * 9 * B // 2)
            for t in range(NT):
                sp.wait_ge(out_qr[t], 16 * B)

        @block.vector
        def _(v):
            nc.vector.memset(pows[:, 0:1], LN_EPS).then_inc(const_ok, 1)
            nc.vector.memset(pows[:, 1:2], -0.5).then_inc(const_ok, 1)
            nc.vector.memset(ones[:], 1.0).then_inc(const_ok, 1)
            v.wait_ge(const_in, 16 * 7)
            nc.vector.tensor_scalar(bias_q[:], qk_bias[:, 0:1], Q_SCALE, None, ALU.mult).then_inc(const_ok, 1)
            nc.vector.tensor_tensor(bias_kl[:], qk_bias[:, 2:3], qk_bias[:, 3:4], ALU.subtract).then_inc(const_ok, 1)
            v.wait_ge(const_ok, 5)
            nc.vector.tensor_tensor(bias_kl[:], bias_kl[:], qk_bias[:, 1:2], ALU.add).then_inc(const_ok, 1)
            nc.vector.tensor_tensor(relx[:], rel[:, :, 0:FAR], rel[:, :, FAR:FAR + 1].to_broadcast([P, H, FAR]),
                                    ALU.subtract).then_inc(const_ok, 1)
            v.sem_inc(const_ok, 1)

            def read_qr(b, t):
                need(v, qr_ps, b, NT, t + 1)
                need(v, out_qr[t], b, 16, 0)
                need(v, qr0_ok, b, NT, t + 1 - NT)
                nc.vector.tensor_copy(QR[t][:, 0:G, :],
                                      b_qr[t % 2][0][:, 0:G * FAR].rearrange("p (h r) -> p h r", r=FAR)
                                      ).then_inc(qr_ev[0], 1)

            def row(b, s, m):
                m_new = m + 1 if s else m
                if own(b):
                    need(v, q_ps, b, 1, 1)
                    need(v, qr_ps, b, NT, -NT)
                    nc.vector.tensor_scalar(T[0][s][:], b_q[:], Q_SCALE, bias_q[:], ALU.mult, ALU.add).then_inc(t_ok[0], 1)
                if new(b):
                    v.wait_ge(x_in[1 - s], m_new * 16 + 16)
                    need(v, mv_ok, b, 1, 1)
                    for t in range(NT):
                        ins = nc.vector.bn_stats(stats[:, t, :], X[1 - s][:, t, :])
                    ins.then_inc(stats_ok, 1)
                if own(b):
                    need(v, t_ok[0], b, 1, 1)
                    need(v, out_sp[s], m, 16 * 9, 0)
                    nc.vector.tensor_copy(SP[0][0][s][:], T[0][s][:]).then_inc(hi_ok[0], 1)
                if new(b):
                    need(v, stats_ok, b, 1, 2)
                    need(v, xn_ok, b, 1, 1)
                    v.sem_inc(stats_go, 1)
                    for t in range(NT):
                        ins = nc.vector.bn_aggr(mv[:, t, :], stats[:, t, :])
                    ins.then_inc(mv_ok, 1)
                if own(b):
                    need(v, hi_ok[0], b, 1, 1)
                    need(v, lo_ok[0], b, 1, 0)
                    nc.vector.tensor_tensor(rest[0][:], T[0][s][:], SP[0][0][s][:], ALU.subtract).then_inc(rest_ok[0], 1)
                    need(v, rest_ok[0], b, 1, 1)
                    nc.vector.tensor_copy(SP[0][1][s][:], rest[0][:]).then_inc(mid_ok[0], 1)
                    read_qr(b, 0)
                if new(b):
                    need(v, rstd_ok, b, 1, 2)
                    if own(b):
                        need(v, out_x[1 - s], m_new, 32, 0)
                    need(v, xnt_ps, b, 1, 0)
                    for t in range(NT):
                        ins = nc.vector.tensor_scalar(XN[1 - s][:, t, :], X[1 - s][:, t, :], mv[:, t, 0:1],
                                                      rstd[:, t:t + 1], ALU.subtract, ALU.mult)
                    ins.then_inc(xn_ok, 1)
                if own(b):
                    read_qr(b, 1)
                    need(v, mid_ok[0], b, 1, 1)
                    nc.vector.tensor_tensor(SP[0][2][s][:], rest[0][:], SP[0][1][s][:], ALU.subtract).then_inc(lo_ok[0], 1)
                    read_qr(b, 2)
                    read_qr(b, 3)

            rows(v, row)

        @block.gpsimd
        def _(g):
            g.wait_ge(const_ok, N_CONST)

            def row(b, s, m):
                m_new = m + 1 if s else m
                if new(b):
                    need(g, xn_ok, b, 1, 1)
                    need(g, mv_ok, b, 1, 2)
                    nc.gpsimd.tensor_tensor(rstd[:], mv[:, :, 1], pows[:, 0:1].to_broadcast([P, NT]), ALU.add
                                            ).then_inc(rstd_add, 1)
                    need(g, rstd_add, b, 1, 2)
                    nc.gpsimd.tensor_tensor(rstd[:], rstd[:], pows[:, 1:2].to_broadcast([P, NT]), ALU.pow).then_inc(rstd_ok, 1)
                if own(b):
                    for n in (1, 2):
                        need(g, t_ok[n], b, 1, 1)
                        need(g, hi_ok[n], b, 1, 1)
                        need(g, lo_ok[n], b, 1, 0)
                        nc.gpsimd.tensor_tensor(rest[n][:], T[n][s][:], SP[n][0][s][:], ALU.subtract).then_inc(rest_ok[n], 1)
                if new(b):
                    g.wait_ge(x_in[1 - s], m_new * 16 + 16)
                    if own(b):
                        need(g, out_x[1 - s], m_new, 32, 0)
                    for t in range(NT):
                        ins = nc.gpsimd.tensor_tensor(Y[1 - s][:, t, :], X[1 - s][:, t, :], bo[:], ALU.add)
                    ins.then_inc(y_ok, 1)
                if own(b):
                    for n in (1, 2):
                        need(g, mid_ok[n], b, 1, 1)
                        nc.gpsimd.tensor_tensor(SP[n][2][s][:], rest[n][:], SP[n][1][s][:], ALU.subtract).then_inc(lo_ok[n], 1)
                    need(g, out_0[s], m, 16, 0)
                    for t in range(NT):
                        for hf in range(2):
                            need(g, qr_ev[hf], b, NT, t + 1)
                        nc.gpsimd.tensor_tensor(QR0[s][:, t, :], QR[t][:, :, 0], ones[:], ALU.mult).then_inc(qr0_ok, 1)

            rows(g, row)

        @block.scalar
        def _(act):
            act.wait_ge(const_in, 16 * 7)
            act.wait_ge(const_ok, N_CONST)

            def read_qr(b, t):
                need(act, qr_ps, b, NT, t + 1)
                need(act, out_qr[t], b, 16, 0)
                need(act, qr0_ok, b, NT, t + 1 - NT)
                nc.scalar.activation(QR[t][:, G:H, :],
                                     b_qr[t % 2][1][:, 0:G * FAR].rearrange("p (h r) -> p h r", r=FAR), ACT.Copy
                                     ).then_inc(qr_ev[1], 1)

            def row(b, s, m):
                if own(b):
                    need(act, k_ps, b, 1, 1)
                    for n, bias in ((1, qk_bias[:, 1:2]), (2, bias_kl[:])):
                        need(act, lo_ok[n], b, 1, -1)
                        nc.scalar.activation(T[n][s][:], b_k[:], ACT.Identity, bias=bias).then_inc(t_ok[n], 1)
                        need(act, out_sp[s], m, 16 * 9, 0)
                        nc.scalar.activation(SP[n][0][s][:], b_k[:], ACT.Identity, bias=bias).then_inc(hi_ok[n], 1)
                    need(act, v_ps, b, 1, 1)
                    need(act, out_v[s], m, 16, 0)
                    nc.scalar.activation(V[s][:], b_v[:].rearrange("p (t e) -> p t e", e=E), ACT.Copy).then_inc(v_ok, 1)
                    for n in (1, 2):
                        read_qr(b, n - 1)
                        need(act, rest_ok[n], b, 1, 1)
                        nc.scalar.activation(SP[n][1][s][:], rest[n][:], ACT.Copy).then_inc(mid_ok[n], 1)
                if new(b):
                    need(act, xnt_ps, b, 1, 2)
                    need(act, v_ps, b, 1, 0)
                    nc.scalar.activation(XNT[1 - s][:], b_xt[:], ACT.Copy).then_inc(xnt_ok, 1)
                if own(b):
                    read_qr(b, 2)
                    read_qr(b, 3)

            rows(act, row)

        @block.tensor
        def _(pe):
            pe.wait_ge(const_in, 16 * 7)
            pe.wait_ge(const_ok, N_CONST)

            def relative(b, s, t):
                for hf in range(2):
                    need(pe, qr_ev[hf], b, NT, t - 1)
                for hf in range(2):
                    ins = nc.tensor.matmul(b_qr[t % 2][hf][:, 0:G * FAR], T[0][s][:, t * P:(t + 1) * P],
                                           relx[:, hf * G:(hf + 1) * G, :], start=True, stop=True)
                ins.then_inc(qr_ps, 1)

            def row(b, s, m):
                if own(b):
                    need(pe, xnt_ok, b, 1, 1)
                    need(pe, t_ok[0], b, 1, 0)
                    nc.tensor.matmul(b_q[:], wq[:], XNT[s][:], start=True, stop=True).then_inc(q_ps, 1)
                    need(pe, hi_ok[2], b, 1, 0)
                    nc.tensor.matmul(b_k[:], wk[:], XNT[s][:], start=True, stop=True).then_inc(k_ps, 1)
                    need(pe, v_ok, b, 1, 0)
                    for t in range(NT):
                        ins = nc.tensor.matmul(b_v[:, t * P:(t + 1) * P], XNT[s][:, t * P:(t + 1) * P], wv[:],
                                               start=True, stop=True)
                    ins.then_inc(v_ps, 1)
                    need(pe, t_ok[0], b, 1, 1)
                    relative(b, s, 0)
                    relative(b, s, 1)
                if new(b):
                    need(pe, xn_ok, b, 1, 2)
                    need(pe, xnt_ok, b, 1, 1)
                    for t in range(NT):
                        ins = nc.tensor.transpose(b_xt[:, t * P:(t + 1) * P], XN[1 - s][:, t, :], ident[:])
                    ins.then_inc(xnt_ps, 1)
                if own(b):
                    relative(b, s, 2)
                    relative(b, s, 3)

            rows(pe, row)


EDGES = (P,) + tuple(n * QBLK - MAX_REL for n in range(1, NQB + 1)) + (0,)
NE = len(EDGES)
NF = FAR
WIDE = P + FAR
MARGIN = 64
PROBS_AT = tuple(par * (MARGIN + P * H * WIDE) + MARGIN for par in range(2))
NJ = 4
WARM = 20
V_COLS = 24 * (NJ - 1) + 32
UNITS = NT * H // NJ
FC = H * NF // P

JOBS = [(u, "probs", j) for u in range(UNITS) for j in range(NJ)]
JOBS += [(u, "features", n) for u in range(2, UNITS, 4) for n in range(2)] + [(7, "out", n) for n in range(2)]
JOBS.sort(key=lambda job: job[0])
OF_ROW_BEFORE = [(0, "probs", j) for j in range(NJ)] + [(2, "features", n) for n in range(2)]
OF_ROW_BEFORE += [(7, "out", n) for n in range(2)]


def jobs_before(b, job, bank=None):
    def count(jobs):
        return sum(bank is None or JOBS.index(x) % 2 == bank for x in jobs)

    earlier = JOBS[:JOBS.index(job)]
    if isinstance(b, int) and b == 0:
        return count([x for x in earlier if x not in OF_ROW_BEFORE])
    if isinstance(b, int) and b == B:
        return B * count(JOBS) - count(OF_ROW_BEFORE) + count([x for x in earlier if x in OF_ROW_BEFORE])
    return b * count(JOBS) - count(OF_ROW_BEFORE) + count(earlier)


def bank_of(job):
    return JOBS.index(job) % 2


def warm_up(nc, bank, ident, count):
    for _ in range(count):
        nc.tensor.matmul(bank, ident, ident, start=True, stop=True)


def attend(nc, w, scr):
    with ExitStack() as ctx:
        def sb(name, shape, dt=F32):
            return ctx.enter_context(nc.sbuf_tensor("a_" + name, shape, dt))

        def ps(name, banks=1):
            return ctx.enter_context(nc.psum_tensor("a_bank_" + name, [P, banks, 512], F32))

        def sem(name):
            return ctx.enter_context(nc.semaphore("a_s_" + name))

        ident = sb("ident", [P, P])
        wo = sb("wo", [P, E])
        v_bias = sb("v_bias", [P, NE, E])
        feat_w = sb("feat_w", [P, FC, P])
        keep = sb("keep", [P, QBLK])
        Q, K, KL = ([sb(f"{n}{s}", [P, G, S], BF16) for s in range(2)] for n in ("q", "k", "kl"))
        v_in = sb("v_in", [P, NT, E])
        V = [sb(f"v{s}", [P, NE, NT, NJ, V_COLS]) for s in range(2)]
        win = [sb(f"win{s}", [P, H, WIN]) for s in range(2)]
        probs = [sb(f"probs{s}", [P, NJ, S + 2 * MAX_REL]) for s in range(2)]
        probs_t = [sb(f"probs_t{s}", [P, NJ, S]) for s in range(2)]
        neg_max = sb("neg_max", [P, NJ])
        sums = sb("sums", [P, NT, H])
        inv = sb("inv", [P, H, HD])
        band = sb("band", [P, WIN])
        beyond = sb("beyond", [P, QBLK - 1])
        left_of = [sb(f"left_of{s}", [P, NT, H]) for s in range(2)]
        left_win = sb("left_win", [P, H, QBLK - 1])
        left = sb("left", [P, H, QBLK])
        feat = sb("feat", [P, H, NF])
        feat_t = sb("feat_t", [P, FC - 1, P])
        last_t = sb("last_t", [P, NT, 2, P])
        att_t = sb("att_t", [P, NT, P])
        y_in = sb("y_in", [P, NT, E])
        o_sb = sb("o_sb", [P, NT, E])
        b_s = ps("s", NJ)
        b_pt = [ps(f"pt{n}") for n in range(2)]
        b_o, b_w = ps("o"), ps("w")

        const_in, const_ok, margin_out = sem("const_in"), sem("const_ok"), sem("margin_out")
        N_CONST_IN, N_CONST_OK = 16 * 8, 6
        ident_in = sem("ident_in")
        STACK = [(n, par, group) for n in range(3) for par in range(2) for group in range(PARTS)]
        SPREAD = [1, 1, 2, 1, 1, 1, 2, 0, 1, 1, 2, 1, 2, 1, 1, 0]
        QK_IN = 16 * len(STACK)
        left_in, win_left, win_band, win_ok = sem("left_in"), sem("win_left"), sem("win_band"), sem("win_ok")
        qk_in, win_in = [sem(f"qk_in{s}") for s in range(2)], [sem(f"win_in{s}") for s in range(2)]
        v_in_ok, v_ok = sem("v_in_ok"), sem("v_ok")
        s_ps, max_ok, exp_ok = sem("s_ps"), sem("max_ok"), sem("exp_ok")
        pt_ps, pt_ev = sem("pt_ps"), [sem("pt_ev0"), sem("pt_ev1")]
        av_ps, w_ps, o_ev, w_ev = sem("av_ps"), sem("w_ps"), sem("o_ev"), sem("w_ev")
        p_out = [[sem(f"p_out{pair}{k}") for k in range(2)] for pair in range(2)]
        f_in, l_in, feat_ok = sem("f_in"), sem("l_in"), sem("feat_ok")
        inv_ok, att_ok = sem("inv_ok"), sem("att_ok")
        y_ld, y_ok, y_st = sem("y_ld"), sem("y_ok"), sem("y_st")
        pool = sem("pool")
        room, go = sem("room"), sem("go")

        def need(eng, sm, b, per_row, c):
            value = b * per_row + c
            if not (isinstance(value, int) and value <= 0):
                eng.wait_ge(sm, value)

        def job_done(eng, b, job):
            need(eng, pt_ps, jobs_before(b, job), 1, 1)

        def bank_free(eng, b, job):
            need(eng, pt_ev[bank_of(job)], jobs_before(b, job, bank_of(job)), 1, 0)

        def job_read(eng, b, job):
            need(eng, pt_ev[bank_of(job)], jobs_before(b, job, bank_of(job)), 1, 1)

        def rows(engine, row):
            row(0, 0, 0, first=True)
            with engine.Fori(0, B // 2 - 1) as i:
                row(i * 2 + 1, 1, i)
                row(i * 2 + 2, 0, i + 1)
            row(B - 1, 1, B // 2 - 1)
            row(B, 0, B // 2, tail=True)

        def between(v):
            whole = v[:]
            return bass.AP(whole.tensor, whole.offset + HD, [whole.ap[0], [V_COLS, NE * NT * NJ], [32, NJ - 1], [1, 24]])

        block = ctx.enter_context(nc.Block())

        @block.sync
        def _(sp):
            flat = win[1][:].rearrange("p h c -> p (h c)")
            sp.dma_start(ident[:], w["ident"]).then_inc(ident_in, 16)
            for dst, src in ((wo[:], w["wo"]), (v_bias[:], w["v_edges"]),
                             (feat_w[:], w["feat_w"]), (keep[:], w["keep"]), (band[:], w["band"]),
                             (beyond[:], w["beyond"]),
                             (flat[:, 0:FC * P].rearrange("p (c e) -> p c e", e=P), w["feat_last"]),
                             (v_in[:, 0, :], w["bv"].partition_broadcast(P))):
                sp.dma_start(dst, src).then_inc(const_in, 16)

            def load_qk(b, s, chosen):
                for n, par, group in chosen:
                    slots = [slot for slot in range(SLOTS) if Q_PART[slot] == group]
                    part, step = (group, 0) if n == 0 else (0, P * S)
                    rows_in = scr["parts"][b, n, part, par * HALF:(par + 1) * HALF]
                    at = par * HALF + slots[0] * HD
                    sp.dma_start((Q, K, KL)[n][s][at:at + len(slots) * HD].rearrange("p g q -> p (g q)"),
                                 bass.AP(rows_in.tensor, rows_in.offset, [[step, len(slots)], [G * S, HD], [1, G * S]])
                                 ).then_inc(qk_in[s], 16)

            def load_left(b, s):
                need(sp, win_ok, b, NT, 1 - NT)
                sp.dma_start(left_of[s][:], scr["qr0"][b]).then_inc(left_in, 16)

            def load_v(b):
                need(sp, v_ok, b, 1, 0)
                sp.dma_start(v_in[:], scr["v"][b]).then_inc(v_in_ok, 16)

            def load_win(b, t, blocks=range(NQB)):
                for n in blocks:
                    own = scr["qr"][b * NT + t, n * QBLK:(n + 1) * QBLK]
                    own = bass.AP(own.tensor, own.offset, [[H * FAR - 1, QBLK], [FAR, H], [1, WIN]])
                    sp.dma_start(win[t % 2][n * QBLK:(n + 1) * QBLK], own).then_inc(win_in[t % 2], 16)

            def row(b, s, m, first=False, tail=False):
                last = isinstance(b, int) and b == B - 1
                for u in range(10 if tail else UNITS):
                    t = u // 4
                    if not tail and u % 4 < 2 and not (last and t == NT - 1):
                        need(sp, s_ps, b, 2 * UNITS, 8 * t)
                        load_win(b + (t == NT - 1), (t + 1) % NT, range(2 * (u % 4), 2 * (u % 4) + 2))
                    if not tail and not last and u == 0:
                        load_left(b + 1, 1 - s)
                        need(sp, s_ps, b, 2 * UNITS, 0)
                    if not tail and not last:
                        done = sum(SPREAD[:u])
                        load_qk(b + 1, 1 - s, STACK[done:done + SPREAD[u]])
                    if not tail and not last and u == 2:
                        load_v(b + 1)
                    if not first and u == 3:
                        need(sp, y_st, b, 16, 0)
                        sp.dma_start(y_in[:], scr["y"][b - 1]).then_inc(y_ld, 16)
                    if not first and u == 9:
                        sp.wait_ge(y_ok, b * 2 + 2)
                        sp.dma_start(scr["y"][b - 1], y_in[:]).then_inc(y_st, 16)
                    if tail:
                        continue
                    for pair in range(2):
                        if u % 4 == 0 and pair == 0:
                            need(sp, f_in, b, 16 * NT, 16 * (t - 1))
                            need(sp, l_in, b, 16 * NT, 16 * (t - 1))
                            sp.sem_inc(room, 1)
                        sp.wait_ge(exp_ok, b * 4 * UNITS + 4 * u + 2 * pair + 2)
                        at = PROBS_AT[t % 2] + (4 * 2 * pair + u % 4) * WIDE
                        sp.dma_start(bass.AP(scr["probs"].tensor, at, [[H * WIDE, P], [4 * WIDE, 2], [1, WIDE]]),
                                     probs[u % 2][:, 2 * pair:2 * pair + 2, t * P:t * P + WIDE]
                                     ).then_inc(p_out[pair][u % 2], 16)
                    if u % 4 == 3:
                        for pair in range(2):
                            for k in range(2):
                                sp.wait_ge(p_out[pair][k], b * 8 * UNITS + 16 * (u // 2 + 1))
                        sp.sem_inc(room, 1)
                        if not (first and t == 0):
                            job_done(sp, b, (4 * t + 2, "features", 1))
                        sp.dma_start(feat[:, :, 1:], bass.AP(scr["probs"].tensor, PROBS_AT[t % 2] + 1,
                                                            [[H * WIDE + 1, P], [WIDE, H], [1, NF - 1]])
                                     ).then_inc(f_in, 16)
                        need(sp, feat_ok, b, NT, t)
                        sp.dma_start(left[:], bass.AP(scr["probs"].tensor, PROBS_AT[t % 2] - QBLK + 1,
                                                     [[H * WIDE + 1, P], [WIDE, H], [1, QBLK]])
                                     ).then_inc(l_in, 16)

            for sm, start in ((y_st, 16), (y_ok, 2)):
                sp.sem_inc(sm, start)
            load_left(0, 0)
            load_win(0, 0)
            load_qk(0, 0, STACK)
            sp.wait_ge(const_ok, N_CONST_OK)
            load_v(0)
            for at in PROBS_AT:
                sp.dma_start(bass.AP(scr["probs"].tensor, at - MARGIN, [[MARGIN, 1], [1, MARGIN]]),
                             probs[0][0:1, 0, 0:MARGIN]).then_inc(margin_out, 16)
            sp.wait_ge(margin_out, 32)
            rows(sp, row)
            sp.wait_ge(y_st, 16 * B + 16)

        @block.tensor
        def _(pe):
            pe.wait_ge(ident_in, 16)
            pe.wait_ge(const_ok, N_CONST_OK)

            def scores(b, u, j, s):
                h, t = 4 * j + u % 4, u // 4
                need(pe, exp_ok, b, 4 * UNITS, 4 * (u - 1) + j + 1)
                pe.sem_inc(go, 1)
                par = slice((h % 2) * HALF, (h % 2) * HALF + ROWS)
                lo, hi = max(t * P - MAX_REL, 0), (t + 1) * P - QBLK - MAX_REL
                first = True
                for keys, a, z in ((KL, 0, lo), (K, hi, S)):
                    if a < z:
                        nc.tensor.matmul(b_s[:, j, a:z], Q[s][par, h // 2, t * P:(t + 1) * P], keys[s][par, h // 2, a:z],
                                         start=first, stop=False, skip_group_check=True)
                        first = False
                for keys in (KL, K):
                    for n in range(NQB):
                        at, edge = t * P + n * QBLK, max(t * P + n * QBLK - MAX_REL, lo)
                        a, z = (lo, edge) if keys is KL else (edge, hi)
                        if a < z:
                            nc.tensor.matmul(b_s[n * QBLK:(n + 1) * QBLK, j, a:z], Q[s][par, h // 2, at:at + QBLK],
                                             keys[s][par, h // 2, a:z], start=False, stop=False, skip_group_check=True)
                for n in range(NQB):
                    edge = t * P + n * QBLK - MAX_REL
                    lo, hi = max(edge, 0), min(edge + WIN, S)
                    ins = nc.tensor.matmul(b_s[n * QBLK:(n + 1) * QBLK, j, lo:hi], ident[:, n * QBLK:(n + 1) * QBLK],
                                           win[t % 2][:, h, lo - edge:hi - edge], start=False, stop=True,
                                           skip_group_check=True)
                if j % 2:
                    ins.then_inc(s_ps, 1)

            def transpose(b, u, j):
                job = (u, "probs", j)
                bank_free(pe, b, job)
                pe.wait_ge(exp_ok, b * 4 * UNITS + 4 * (u - 1) + j + 1)
                for t in range(NT):
                    ins = nc.tensor.transpose(b_pt[bank_of(job)][:, 0, t * P:(t + 1) * P],
                                              probs[(u - 1) % 2][:, j, MAX_REL + t * P:MAX_REL + (t + 1) * P],
                                              ident[:])
                ins.then_inc(pt_ps, 1)

            def attended(b, u, s):
                t, hh = u // 4, u % 4
                after = (b, u + 1) if u < UNITS - 1 else (b + 1, 0)
                for j in (2, 3):
                    job_read(pe, after[0], (after[1], "probs", j))
                if u == 0:
                    pe.wait_ge(v_ok, b + 1)
                    need(pe, o_ev, b, 1, 0)
                first = hh == 0
                for kt in range(NT):
                    if kt == t:
                        parts = [(n * QBLK, (n + 1) * QBLK, EDGES.index(max(n * QBLK - MAX_REL, 0)))
                                 for n in range(NQB)]
                    elif kt == t - 1:
                        parts = [(0, QBLK, EDGES.index(P - MAX_REL)), (QBLK, P, EDGES.index(P))]
                    else:
                        parts = [(0, P, EDGES.index(P if kt < t else 0))]
                    for lo, hi, edge in parts:
                        for j in range(NJ):
                            ins = nc.tensor.matmul(b_o[32 * j:32 * j + 32, 0, t * P + lo:t * P + hi],
                                                   V[s][:, edge, kt, j, hh * 24:hh * 24 + 32],
                                                   probs_t[u % 2][:, j, kt * P + lo:kt * P + hi],
                                                   start=first, stop=False, skip_group_check=True)
                        first = False
                ins.then_inc(av_ps, 1)

            def features(b, u):
                job, nxt = (u, "features", 0), (u, "features", 1)
                flat = feat[:].rearrange("p h f -> p (h f)")
                pe.wait_ge(feat_ok, b * NT + (u - 2) // 4)
                bank_free(pe, b, job)
                for c in range(FC - 1):
                    ins = nc.tensor.transpose(b_pt[bank_of(job)][:, 0, c * P:(c + 1) * P],
                                              flat[:, c * P:(c + 1) * P], ident[:])
                ins.then_inc(pt_ps, 1)
                pe.wait_ge(inv_ok, b * NT + (u - 2) // 4)
                bank_free(pe, b, nxt)
                nc.tensor.transpose(b_pt[bank_of(nxt)][:, 0, 0:P], flat[:, (FC - 1) * P:], ident[:])
                nc.tensor.transpose(b_pt[bank_of(nxt)][:, 0, P:2 * P], inv[:].rearrange("p h d -> p (h d)"),
                                    ident[:]).then_inc(pt_ps, 1)

            def weigh(b, u):
                t = ((u - 3) // 4 - 1) % NT
                for n in range(2):
                    job_read(pe, b, (u - 1, "features", n))
                if t == 0:
                    need(pe, w_ev, b, 1, 0)
                for c in range(FC):
                    ins = nc.tensor.matmul(b_w[:, 0, t * P:(t + 1) * P], feat_w[:, c, :],
                                           feat_t[:, c, :] if c < FC - 1 else last_t[:, t, 0, :],
                                           start=c == 0, stop=c == FC - 1)
                ins.then_inc(w_ps, 1)

            def project(b):
                pe.wait_ge(att_ok, b)
                for n in range(2):
                    job = (7, "out", n)
                    bank_free(pe, b, job)
                    for t in (2 * n, 2 * n + 1):
                        ins = nc.tensor.matmul(b_pt[bank_of(job)][:, 0, (t % 2) * P:(t % 2 + 1) * P],
                                               att_t[:, t, :], wo[:], start=True, stop=True)
                    ins.then_inc(pt_ps, 1)

            def row(b, s, m, first=False, tail=False):
                for u in range(8 if tail else UNITS):
                    if u == 0 and not tail:
                        pe.wait_ge(qk_in[s], m * QK_IN + QK_IN)
                    if u % 4 == 0 and not tail:
                        pe.wait_ge(win_ok, b * NT + u // 4 + 1)
                    for pair in ((0, 1), (2, 3)):
                        for j in pair:
                            if not tail:
                                scores(b, u, j, s)
                        for j in pair:
                            if (u and not tail) or (u == 0 and not first):
                                transpose(b, u, j)
                    if u > 1 and not tail:
                        attended(b, u - 2, s)
                        if first and u == 3:
                            warm_up(nc, b_w[:, 0, 0:P], ident[:], WARM)
                    elif u < 2 and not first:
                        attended(b - 1, u + UNITS - 2, 1 - s)
                    if u % 4 == 2 and not (first if u == 2 else tail):
                        features(b, u)
                    if u % 4 == 3 and not (first if u == 3 else tail):
                        weigh(b, u)
                    if u == 7 and not first:
                        project(b)

            rows(pe, row)

        @block.vector
        def _(v):
            flat = win[1][:].rearrange("p h c -> p (h c)")
            nc.vector.memset(between(V[0]), 0.0).then_inc(const_ok, 1)
            for half in probs:
                nc.vector.memset(half[:, :, 0:MARGIN], 0.0)
                nc.vector.memset(half[:, :, MAX_REL + S:], 0.0).then_inc(const_ok, 1)
            v.wait_ge(const_in, N_CONST_IN)
            nc.vector.tensor_tensor(v_bias[:], v_bias[:], v_in[:, 0:1, :].to_broadcast([P, NE, E]),
                                    ALU.add).then_inc(const_ok, 1)
            nc.vector.tensor_tensor(feat_w[:], feat_w[:], flat[:, 0:FC * P].rearrange("p (c e) -> p c e", e=P),
                                    ALU.subtract).then_inc(const_ok, 1)

            def read_probs(b, u, j):
                job = (u, "probs", j)
                job_done(v, b, job)
                need(v, av_ps, b, UNITS, u - 2)
                nc.vector.tensor_copy(probs_t[(u - 1) % 2][:, j, :], b_pt[bank_of(job)][:, 0, :]
                                      ).then_inc(pt_ev[bank_of(job)], 1)

            def row(b, s, m, first=False, tail=False):
                for u in range(8 if tail else UNITS):
                    for pair in range(2):
                        if not tail:
                            v.wait_ge(s_ps, b * 2 * UNITS + 2 * u + pair + 1)
                            need(v, exp_ok, b, 4 * UNITS, 4 * (u - 1) + 2 * pair + 2)
                            nc.vector.tensor_reduce(neg_max[:, 2 * pair:2 * pair + 2], b_s[:, 2 * pair:2 * pair + 2, :],
                                                    AX.X, ALU.max, negate=True).then_inc(max_ok, 1)
                        if (u and not tail) or (u == 0 and not first):
                            read_probs(b, u, 2 * pair + 1)
                    if u % 4 == 1 and not (first if u == 1 else tail):
                        t = (u // 4 - 1) % NT
                        need(v, exp_ok, b, 4 * UNITS, 4 * (u - 1))
                        if not (isinstance(b, int) and b == 0 and u == 5):
                            job_done(v, b if u > 1 else b - 1, ((u - 3) % UNITS, "features", 1))
                        nc.vector.reciprocal(inv[:], sums[:, t, :].rearrange("p (h o) -> p h o", o=1)
                                             .to_broadcast([P, H, HD])).then_inc(inv_ok, 1)
                    if u % 4 == 2 and not (first if u == 2 else tail):
                        job = (u, "features", 1)
                        t = (u // 4 - 1) % NT
                        job_done(v, b, job)
                        if t == 0:
                            need(v, att_ok, b, 1, 0)
                        nc.vector.tensor_copy(last_t[:, t].rearrange("p a q -> p (a q)"),
                                              b_pt[bank_of(job)][:, 0, 0:2 * P]).then_inc(pt_ev[bank_of(job)], 1)
                    if u == 4 and not first:
                        v.wait_ge(w_ps, b * NT)
                        v.wait_ge(o_ev, b)
                        if not (isinstance(b, int) and b == 1):
                            job_done(v, b - 1, (7, "out", 1))
                        nc.vector.tensor_tensor(att_t[:], o_sb[:], b_w[:, 0, :].rearrange("p (t q) -> p t q", q=P),
                                                ALU.add).then_inc(w_ev, 1)
                        v.wait_ge(w_ev, b)
                        job_read(v, b, (2, "features", 1))
                        nc.vector.tensor_tensor(att_t[:], att_t[:], last_t[:, :, 1, :], ALU.mult).then_inc(att_ok, 1)
                    if u == 7 and not first:
                        job = (7, "out", 1)
                        job_done(v, b, job)
                        v.wait_ge(y_ld, b * 16)
                        nc.vector.tensor_tensor(y_in[:, 2:4, :], y_in[:, 2:4, :],
                                                b_pt[bank_of(job)][:, 0, 0:2 * P].rearrange("p (t e) -> p t e", e=E),
                                                ALU.add).then_inc(pt_ev[bank_of(job)], 1)
                        job_read(v, b, job)
                        v.sem_inc(y_ok, 1)

            rows(v, row)

        @block.scalar
        def _(act):
            act.wait_ge(const_ok, N_CONST_OK)
            act.wait_ge(margin_out, 32)

            def read_probs(b, u, j):
                job = (u, "probs", j)
                job_done(act, b, job)
                need(act, av_ps, b, UNITS, u - 2)
                nc.scalar.activation(probs_t[(u - 1) % 2][:, j, :], b_pt[bank_of(job)][:, 0, :], ACT.Copy
                                     ).then_inc(pt_ev[bank_of(job)], 1)

            def row(b, s, m, first=False, tail=False):
                for u in range(8 if tail else UNITS):
                    t = u // 4
                    for pair in range(2):
                        if (u and not tail) or (u == 0 and not first):
                            read_probs(b, u, 2 * pair)
                        if tail:
                            continue
                        act.wait_ge(max_ok, b * 2 * UNITS + 2 * u + pair + 1)
                        need(act, p_out[pair][u % 2], b, 8 * UNITS, 16 * (u // 2))
                        if u % 4 == 0:
                            need(act, inv_ok, b, NT, t + 1 - NT)
                        for j in (2 * pair, 2 * pair + 1):
                            if u > 1 or u and not first:
                                job_done(act, b, (u - 1, "probs", j))
                            elif not first:
                                job_done(act, b - 1, (UNITS - 1, "probs", j))
                            h = 4 * j + u % 4
                            nc.scalar.activation(probs[u % 2][:, j, MAX_REL:MAX_REL + S], b_s[:, j, :], ACT.Exp,
                                                 bias=neg_max[:, j:j + 1], accum_out=sums[:, t, h:h + 1]
                                                 ).then_inc(exp_ok, 1)
                    if u == 1 and not first:
                        act.wait_ge(av_ps, b * UNITS)
                        need(act, y_ok, b, 2, 0)
                        nc.scalar.activation(o_sb[:], b_o[:, 0, :].rearrange("p (t q) -> p t q", q=P), ACT.Copy
                                             ).then_inc(o_ev, 1)
                    if u % 4 == 2 and not (first if u == 2 else tail):
                        job = (u, "features", 0)
                        job_done(act, b, job)
                        need(act, w_ps, b, NT, u // 4 - 1)
                        nc.scalar.activation(feat_t[:], b_pt[bank_of(job)][:, 0, :].rearrange("p (c q) -> p c q", q=P),
                                             ACT.Copy).then_inc(pt_ev[bank_of(job)], 1)
                    if u == 7 and not first:
                        job = (7, "out", 0)
                        job_done(act, b, job)
                        act.wait_ge(w_ev, b)
                        nc.scalar.activation(o_sb[:, 0:2, :], b_pt[bank_of(job)][:, 0, 0:2 * P]
                                             .rearrange("p (t e) -> p t e", e=E), ACT.Copy
                                             ).then_inc(pt_ev[bank_of(job)], 1)

            rows(act, row)

        @block.gpsimd
        def _(g):
            nc.gpsimd.memset(between(V[1]), 0.0).then_inc(const_ok, 1)
            g.wait_ge(const_ok, N_CONST_OK)

            def make_v(b, kt, s):
                if kt == 0:
                    g.wait_ge(v_in_ok, b * 16 + 16)
                    need(g, av_ps, b, UNITS, -UNITS)
                for e in range(NE):
                    one = V[s][:, e, kt]
                    part, (sj, nj) = one.ap[0], one.ap[1]
                    out = bass.AP(one.tensor, one.offset, [part, [sj, nj], [32, NJ], [1, HD]])
                    ins = nc.gpsimd.tensor_tensor(out, v_in[:, kt, :].rearrange("p (j h d) -> p j h d", j=NJ, d=HD),
                                                  v_bias[:, e, :].rearrange("p (j h d) -> p j h d", j=NJ, d=HD), ALU.add)
                if kt == NT - 1:
                    ins.then_inc(v_ok, 1)

            def make_feature(b, t):
                at = 5 * (b * NT + t)
                g.wait_ge(l_in, b * 16 * NT + 16 * (t + 1))
                nc.gpsimd.tensor_tensor(left[:], left[:], keep[:].rearrange("p (o c) -> p o c", o=1)
                                        .to_broadcast([P, H, QBLK]), ALU.mult).then_inc(pool, 1)
                n = QBLK // 2
                for k in range(4):
                    g.wait_ge(pool, at + k + 1)
                    nc.gpsimd.tensor_tensor(left[:, :, 0:n], left[:, :, 0:n], left[:, :, n:2 * n], ALU.add).then_inc(pool, 1)
                    n //= 2
                g.wait_ge(pool, at + 5)
                g.wait_ge(f_in, b * 16 * NT + 16 * (t + 1))
                nc.gpsimd.tensor_tensor(feat[:, :, 0:1], left[:, :, 0:1], left[:, :, 1:2], ALU.add).then_inc(feat_ok, 1)

            def make_window(b, t, s):
                own, places = win[t % 2][:], QBLK - 1
                g.wait_ge(left_in, b * 16 + 16)
                need(g, win_ok, b, NT, t)
                nc.gpsimd.tensor_tensor(left_win[:], left_of[s][:, t, :].rearrange("p (h o) -> p h o", o=1)
                                        .to_broadcast([P, H, places]),
                                        beyond[:].rearrange("p (o c) -> p o c", o=1).to_broadcast([P, H, places]),
                                        ALU.mult).then_inc(win_left, 1)
                g.wait_ge(win_in[t % 2], b * 128 + 64 * (t // 2 + 1))
                nc.gpsimd.tensor_tensor(own, own, band[:].rearrange("p (o c) -> p o c", o=1).to_broadcast([P, H, WIN]),
                                        ALU.mult).then_inc(win_band, 1)
                need(g, win_left, b, NT, t + 1)
                need(g, win_band, b, NT, t + 1)
                nc.gpsimd.tensor_tensor(own[:, :, 0:places], own[:, :, 0:places], left_win[:], ALU.add).then_inc(win_ok, 1)

            make_window(0, 0, 0)
            for kt in range(NT):
                make_v(0, kt, 0)

            def row(b, s, m, first=False, tail=False):
                last = isinstance(b, int) and b == B - 1
                if not first:
                    make_feature(b - 1, NT - 1)
                for t in range(NT - 1 if not tail else 0):
                    make_window(b, t + 1, s)
                    if not last:
                        make_v(b + 1, t, 1 - s)
                    if t == 1 and not first:
                        add_out(b)
                    make_feature(b, t)
                if not tail and not last:
                    make_window(b + 1, 0, 1 - s)
                    make_v(b + 1, NT - 1, 1 - s)
                if tail:
                    add_out(b)

            def add_out(b):
                job_read(g, b, (7, "out", 0))
                g.wait_ge(y_ld, b * 16)
                nc.gpsimd.tensor_tensor(y_in[:, 0:2, :], y_in[:, 0:2, :], o_sb[:, 0:2, :], ALU.add).then_inc(y_ok, 1)

            rows(g, row)


H2, D2 = 4, 32
MIX_JOBS = [(u, "probs", j) for u in range(NT) for j in range(H2)]
MIX_OLD = [(0, "probs", j) for j in range(H2)] + [(1, "inv", 0), (3, "out", 0)]
MIX_NEW = [(1, "nx", 0), (2, "q", 0), (2, "k", 0), (3, "v", 0)]
for _new in ((1, "inv", 0), (1, "nx", 0), (2, "q", 0), (2, "k", 0), (3, "v", 0), (3, "out", 0)):
    MIX_JOBS.append(_new)
MIX_JOBS.sort(key=lambda job: job[0])


def mix_jobs_before(b, job, bank=None):
    def count(jobs):
        return sum(bank is None or MIX_JOBS.index(x) % 2 == bank for x in jobs)

    def of_row(n):
        return [x for x in MIX_JOBS if not (n in (-1, 0) and x in MIX_OLD or n in (B - 1, B) and x in MIX_NEW
                                            or n in (-1, B) and x not in MIX_OLD + MIX_NEW)]

    earlier = MIX_JOBS[:MIX_JOBS.index(job)]
    if isinstance(b, int):
        return sum(count(of_row(n)) for n in range(-1, b)) + count([x for x in earlier if x in of_row(b)])
    return b * count(MIX_JOBS) + count(of_row(-1)) - count(MIX_OLD) + count(earlier)


def mix(nc, w, scr):
    with ExitStack() as ctx:
        def sb(name, shape, dt=F32):
            return ctx.enter_context(nc.sbuf_tensor("m_" + name, shape, dt))

        def ps(name, banks=1):
            return ctx.enter_context(nc.psum_tensor("m_bank_" + name, [P, banks, 512], F32))

        def sem(name):
            return ctx.enter_context(nc.semaphore("m_s_" + name))

        ident, wq, wk, wo = (sb(n, [P, P]) for n in ("ident", "wq", "wk", "wo"))
        wv = sb("wv", [P, D2])
        g1 = sb("g1", [P, 1])
        pows = sb("pows", [P, 1])
        ones = sb("ones", [P, NT * H2 * D2])
        xn = sb("xn", [P, NT, E])
        nx = sb("nx", [P, NT, E])
        square = sb("square", [P, E])
        mean_sq = sb("mean_sq", [P, NT])
        rms = sb("rms", [P, NT])
        nx_t = sb("nx_t", [P, S])
        Q, K = ([sb(f"{n}{s}", [P, S]) for s in range(2)] for n in ("q", "k"))
        V = [sb(f"v{s}", [P, NT, D2]) for s in range(2)]
        probs = sb("probs", [P, H2, S])
        probs_t = [sb(f"probs_t{s}", [P, H2, S]) for s in range(2)]
        neg_max = sb("neg_max", [P, H2])
        sums = [sb(f"sums{s}", [P, NT, H2]) for s in range(2)]
        inv = sb("inv", [P, NT, H2])
        inv_wide = sb("inv_wide", [P, NT, H2, D2])
        inv_t = sb("inv_t", [P, S])
        att_t = sb("att_t", [P, NT, P])
        xo = sb("xo", [P, NT, E])
        b_s = ps("s", H2)
        b_pt = [ps(f"pt{n}") for n in range(2)]
        b_o = [ps(f"o{s}") for s in range(2)]

        const_in, const_ok = sem("const_in"), sem("const_ok")
        N_IN = 16 * 6
        xn_in, sq_ok, ms_ok, rms_ok, nx_ok = sem("xn_in"), sem("sq_ok"), sem("ms_ok"), sem("rms_ok"), sem("nx_ok")
        s_ps, max_ok, exp_ok = sem("s_ps"), sem("max_ok"), sem("exp_ok")
        pt_ps, pt_ev = sem("pt_ps"), [sem("pt_ev0"), sem("pt_ev1")]
        av_ps, inv_ok, wide_ok, att_ok = sem("av_ps"), sem("inv_ok"), sem("wide_ok"), sem("att_ok")
        xo_in, xo_out = sem("xo_in"), sem("xo_out")

        def need(eng, sm, b, per_row, c):
            value = b * per_row + c
            if not (isinstance(value, int) and value <= 0):
                eng.wait_ge(sm, value)

        def bank_of(job):
            return MIX_JOBS.index(job) % 2

        def job_done(eng, b, job):
            need(eng, pt_ps, mix_jobs_before(b, job), 1, 1)

        def bank_free(eng, b, job):
            need(eng, pt_ev[bank_of(job)], mix_jobs_before(b, job, bank_of(job)), 1, 0)

        def job_read(eng, b, job):
            need(eng, pt_ev[bank_of(job)], mix_jobs_before(b, job, bank_of(job)), 1, 1)

        def rows(engine, row):
            row(-1, 1, "lead")
            row(0, 0, "first")
            with engine.Fori(0, B // 2 - 1) as i:
                row(i * 2 + 1, 1, "")
                row(i * 2 + 2, 0, "")
            row(B - 1, 1, "last")
            row(B, 0, "tail")

        def parts(kind):
            return kind not in ("lead", "tail"), kind not in ("lead", "first"), kind not in ("last", "tail")

        block = ctx.enter_context(nc.Block())

        @block.sync
        def _(sp):
            for dst, src in ((ident[:], w["ident"]), (wq[:], w["m_wq"]), (wk[:], w["m_wk"]), (wo[:], w["m_wo"]),
                             (wv[:], w["m_wv"]), (g1[:], w["g1"])):
                sp.dma_start(dst, src).then_inc(const_in, 16)
            for sm, start in ((xo_out, 16), (wide_ok, 1), (inv_ok, 1), (att_ok, 1)):
                sp.sem_inc(sm, start)

            def row(b, s, kind):
                own, old, new = parts(kind)
                if new:
                    need(sp, nx_ok, b, 1, 1)
                    sp.dma_start(xn[:], scr["xn"][b + 1]).then_inc(xn_in, 16)
                if old:
                    need(sp, xo_out, b, 16, 0)
                    sp.dma_start(xo[:], scr["xn"][b - 1]).then_inc(xo_in, 16)
                    job_read(sp, b, (3, "out", 0))
                    sp.dma_start(scr["x1"][b - 1], xo[:]).then_inc(xo_out, 16)

            rows(sp, row)
            sp.wait_ge(xo_out, 16 * B + 16)

        @block.tensor
        def _(pe):
            pe.wait_ge(const_in, N_IN)

            def small(b, s, u, what):
                job = (u, what, 0)
                bank = b_pt[bank_of(job)]
                bank_free(pe, b, job)
                if what == "inv":
                    pe.wait_ge(wide_ok, b + 1)
                    for t in range(NT):
                        ins = nc.tensor.transpose(bank[:, 0, t * P:(t + 1) * P],
                                                  inv_wide[:, t].rearrange("p h d -> p (h d)"), ident[:])
                elif what == "nx":
                    need(pe, nx_ok, b, 1, 2)
                    for t in range(NT):
                        ins = nc.tensor.transpose(bank[:, 0, t * P:(t + 1) * P], nx[:, t, :], ident[:])
                elif what in ("q", "k"):
                    job_read(pe, b, (1, "nx", 0))
                    ins = nc.tensor.matmul(bank[:, 0, :], (wq if what == "q" else wk)[:], nx_t[:], start=True, stop=True)
                elif what == "v":
                    for t in range(NT):
                        ins = nc.tensor.matmul(bank[:, 0, t * D2:(t + 1) * D2], nx_t[:, t * P:(t + 1) * P], wv[:],
                                               start=True, stop=True)
                else:
                    pe.wait_ge(att_ok, b + 1)
                    for t in range(NT):
                        ins = nc.tensor.matmul(bank[:, 0, t * P:(t + 1) * P], att_t[:, t, :], wo[:], start=True, stop=True)
                ins.then_inc(pt_ps, 1)

            def attended(b, u, s):
                after = (b, u + 1) if u < NT - 1 else (b + 1, 0)
                for j in (2, 3):
                    job_read(pe, after[0], (after[1], "probs", j))
                if u == 0:
                    need(pe, att_ok, b, 1, 0)
                for kt in range(NT):
                    for h in range(H2):
                        ins = nc.tensor.matmul(b_o[s][32 * h:32 * h + 32, 0, u * P:(u + 1) * P], V[s][:, kt, :],
                                               probs_t[u % 2][:, h, kt * P:(kt + 1) * P],
                                               start=kt == 0, stop=kt == NT - 1, skip_group_check=True)
                ins.then_inc(av_ps, 1)

            def row(b, s, kind):
                own, old, new = parts(kind)
                for u in range(NT):
                    if u == 0 and own:
                        for job in ((2, "q", 0), (2, "k", 0), (3, "v", 0)):
                            job_read(pe, b - 1, job)
                    for pair in ((0, 1), (2, 3)):
                        if own:
                            for h in pair:
                                need(pe, exp_ok, b, 4 * NT, 4 * (u - 1) + h + 1)
                                ins = nc.tensor.matmul(b_s[:, h, :], Q[s][h * D2:(h + 1) * D2, u * P:(u + 1) * P],
                                                       K[s][h * D2:(h + 1) * D2, :], start=True, stop=True)
                            ins.then_inc(s_ps, 1)
                        if (own and u) or (old and not u):
                            for j in pair:
                                job = (u, "probs", j)
                                bank_free(pe, b, job)
                                pe.wait_ge(exp_ok, b * 4 * NT + 4 * (u - 1) + j + 1)
                                for t in range(NT):
                                    ins = nc.tensor.transpose(b_pt[bank_of(job)][:, 0, t * P:(t + 1) * P],
                                                              probs[:, j, t * P:(t + 1) * P], ident[:])
                                ins.then_inc(pt_ps, 1)
                    if u > 1 and own:
                        attended(b, u - 2, s)
                    elif u < 2 and old:
                        attended(b - 1, u + NT - 2, 1 - s)
                    for what, at, wanted in (("inv", 1, old), ("nx", 1, new), ("q", 2, new), ("k", 2, new),
                                             ("v", 3, new), ("out", 3, old)):
                        if at == u and wanted:
                            small(b, s, u, what)

            rows(pe, row)

        @block.vector
        def _(v):
            nc.vector.memset(pows[:], -0.5).then_inc(const_ok, 1)
            nc.vector.memset(ones[:], 1.0).then_inc(const_ok, 1)
            v.wait_ge(const_in, N_IN)

            def row(b, s, kind):
                own, old, new = parts(kind)
                for u in range(NT):
                    for pair in range(2):
                        if own:
                            v.wait_ge(s_ps, b * 2 * NT + 2 * u + pair + 1)
                            need(v, exp_ok, b, 4 * NT, 4 * (u - 1) + 2 * pair + 2)
                            nc.vector.tensor_reduce(neg_max[:, 2 * pair:2 * pair + 2], b_s[:, 2 * pair:2 * pair + 2, :],
                                                    AX.X, ALU.max, negate=True).then_inc(max_ok, 1)
                        if (own and u) or (old and not u):
                            job = (u, "probs", 2 * pair + 1)
                            job_done(v, b, job)
                            need(v, av_ps, b, NT, u - 2)
                            nc.vector.tensor_copy(probs_t[(u - 1) % 2][:, 2 * pair + 1, :], b_pt[bank_of(job)][:, 0, :]
                                                  ).then_inc(pt_ev[bank_of(job)], 1)
                        if u == 1 and pair == 0 and new:
                            need(v, sq_ok, b, NT, 2 * NT)
                            need(v, rms_ok, b, 1, 1)
                            need(v, nx_ok, b, 1, 1)
                            nc.vector.tensor_scalar(rms[:], mean_sq[:], 1.0 / E, RMS_EPS, ALU.mult, ALU.add
                                                    ).then_inc(ms_ok, 1)
                    if u == 0 and old:
                        v.wait_ge(exp_ok, b * 4 * NT)
                        need(v, wide_ok, b, 1, 0)
                        nc.vector.reciprocal(inv[:], sums[1 - s][:]).then_inc(inv_ok, 1)
                    if u == 1 and new:
                        need(v, rms_ok, b, 1, 2)
                        if kind != "lead":
                            job_done(v, b - 1, (1, "nx", 0))
                        for t in range(NT):
                            ins = nc.vector.tensor_scalar(nx[:, t, :], xn[:, t, :], rms[:, t:t + 1], None, ALU.mult)
                        ins.then_inc(nx_ok, 1)
                    if u == 1 and new:
                        job = (1, "nx", 0)
                        job_done(v, b, job)
                        if kind != "lead":
                            job_done(v, b - 1, (3, "v", 0))
                        nc.vector.tensor_scalar(nx_t[:], b_pt[bank_of(job)][:, 0, :], g1[:], None, ALU.mult
                                                ).then_inc(pt_ev[bank_of(job)], 1)
                    if u == 2 and old:
                        job_read(v, b, (1, "inv", 0))
                        v.wait_ge(av_ps, b * NT)
                        if not (isinstance(b, int) and b == 1):
                            job_done(v, b - 1, (3, "out", 0))
                        nc.vector.tensor_tensor(att_t[:].rearrange("p t q -> p (t q)"), b_o[1 - s][:, 0, :], inv_t[:], ALU.mult
                                                ).then_inc(att_ok, 1)
                    if u == 2 and new:
                        job = (2, "k", 0)
                        job_done(v, b, job)
                        need(v, s_ps, b, 2 * NT, 0)
                        nc.vector.tensor_copy(K[1 - s][:], b_pt[bank_of(job)][:, 0, :]).then_inc(pt_ev[bank_of(job)], 1)
                    if u == 3 and old:
                        job = (3, "out", 0)
                        job_done(v, b, job)
                        v.wait_ge(xo_in, b * 16)
                        nc.vector.tensor_tensor(xo[:], xo[:], b_pt[bank_of(job)][:, 0, :]
                                                .rearrange("p (t e) -> p t e", e=E), ALU.add
                                                ).then_inc(pt_ev[bank_of(job)], 1)

            rows(v, row)

        @block.gpsimd
        def _(g):
            g.wait_ge(const_ok, 2)

            def row(b, s, kind):
                own, old, new = parts(kind)
                if new:
                    need(g, ms_ok, b, 1, 2)
                    nc.gpsimd.tensor_tensor(rms[:], rms[:], pows[:].to_broadcast([P, NT]), ALU.pow).then_inc(rms_ok, 1)
                if old:
                    g.wait_ge(inv_ok, b + 1)
                    if not (isinstance(b, int) and b == 1):
                        job_done(g, b - 1, (1, "inv", 0))
                    nc.gpsimd.tensor_tensor(inv_wide[:], inv[:].rearrange("p t (h o) -> p t h o", o=1)
                                            .to_broadcast([P, NT, H2, D2]),
                                            ones[:].rearrange("p (t h d) -> p t h d", t=NT, h=H2), ALU.mult
                                            ).then_inc(wide_ok, 1)

            rows(g, row)

        @block.scalar
        def _(act):
            act.wait_ge(const_in, N_IN)

            def row(b, s, kind):
                own, old, new = parts(kind)
                for u in range(NT):
                    for pair in range(2):
                        if (own and u) or (old and not u):
                            job = (u, "probs", 2 * pair)
                            job_done(act, b, job)
                            need(act, av_ps, b, NT, u - 2)
                            nc.scalar.activation(probs_t[(u - 1) % 2][:, 2 * pair, :], b_pt[bank_of(job)][:, 0, :],
                                                 ACT.Copy).then_inc(pt_ev[bank_of(job)], 1)
                        if not own:
                            continue
                        act.wait_ge(max_ok, b * 2 * NT + 2 * u + pair + 1)
                        if u == 0:
                            need(act, inv_ok, b, 1, 0)
                        for j in (2 * pair, 2 * pair + 1):
                            if u or old:
                                job_done(act, b, (u, "probs", j))
                            nc.scalar.activation(probs[:, j, :], b_s[:, j, :], ACT.Exp, bias=neg_max[:, j:j + 1],
                                                 accum_out=sums[s][:, u, j:j + 1]).then_inc(exp_ok, 1)
                    if u == 0 and new:
                        need(act, xn_in, b, 16, 32)
                        need(act, ms_ok, b, 1, 1)
                        for t in range(NT):
                            need(act, sq_ok, b, NT, NT + t)
                            nc.scalar.activation(square[:], xn[:, t, :], ACT.Square, accum_out=mean_sq[:, t:t + 1]
                                                 ).then_inc(sq_ok, 1)
                    if u == 1 and old:
                        job = (1, "inv", 0)
                        job_done(act, b, job)
                        need(act, att_ok, b, 1, 0)
                        nc.scalar.activation(inv_t[:], b_pt[bank_of(job)][:, 0, :], ACT.Copy
                                             ).then_inc(pt_ev[bank_of(job)], 1)
                    if u == 2 and new:
                        job = (2, "q", 0)
                        job_done(act, b, job)
                        need(act, s_ps, b, 2 * NT, 0)
                        nc.scalar.activation(Q[1 - s][:], b_pt[bank_of(job)][:, 0, :], ACT.Copy, scale=D2 ** -0.5
                                             ).then_inc(pt_ev[bank_of(job)], 1)
                    if u == 3 and new:
                        job = (3, "v", 0)
                        job_done(act, b, job)
                        need(act, av_ps, b, NT, 0)
                        nc.scalar.activation(V[1 - s][:], b_pt[bank_of(job)][:, 0, 0:NT * D2]
                                             .rearrange("p (t d) -> p t d", d=D2), ACT.Copy
                                             ).then_inc(pt_ev[bank_of(job)], 1)

            rows(act, row)


NX = 8
FFN = [NX] + list(range(NX))
NEXP = NX + 1
TAKEN = -4.0


def experts(nc, w, scr, out):
    with ExitStack() as ctx:
        def sb(name, shape, dt=F32):
            return ctx.enter_context(nc.sbuf_tensor("e_" + name, shape, dt))

        def ps(name):
            return ctx.enter_context(nc.psum_tensor("e_bank_" + name, [P, 512], F32))

        def sem(name):
            return ctx.enter_context(nc.semaphore("e_s_" + name))

        ident = sb("ident", [P, P])
        w1, w3, w2 = (sb(n, [P, NEXP, P]) for n in ("w1", "w3", "w2"))
        wr = sb("wr", [P, NX])
        g2 = sb("g2", [P, 1])
        r_bias, rank = sb("r_bias", [P, NX]), sb("rank", [P, NX])
        minus_half, euler = sb("minus_half", [P, 1]), sb("euler", [P, 1])
        x1 = [sb(f"x1{s}", [P, NT, E]) for s in range(2)]
        y = [sb(f"y{s}", [P, NT, E]) for s in range(2)]
        nx = sb("nx", [P, NT, E])
        square = sb("square", [P, E])
        mean_sq, rms = sb("mean_sq", [P, NT]), sb("rms", [P, NT])
        nx_t = [sb(f"nx_t{s}", [P, S]) for s in range(2)]
        probs, eq, rest, one0, one1 = (sb("r_" + n, [P, NT, NX]) for n in ("probs", "eq", "rest", "one0", "one1"))
        top, total, top0, top1, key, w_0, w_1 = (sb("c_" + n, [P, NT]) for n in (
            "top", "total", "top0", "top1", "key", "w_0", "w_1"))
        comb = [sb(f"comb{s}", [P, NT, NX]) for s in range(2)]
        gate = [sb(f"gate{n}", [P, S]) for n in range(2)]
        hid = [sb(f"hid{n}", [P, S]) for n in range(2)]
        b_g, b_u, b_y = ([ps(f"{c}{n}") for n in range(2)] for c in "guy")
        b_t, b_r = ps("t"), ps("r")

        const_in, const_ok = sem("const_in"), sem("const_ok")
        N_IN = 16 * 5
        weights_in = sem("weights_in")
        x_in, y_in, stored = sem("x_in"), sem("y_in"), sem("stored")
        sq_ok, ms_ok, rms_ok, nx_ok = sem("sq_ok"), sem("ms_ok"), sem("rms_ok"), sem("nx_ok")
        t_ps, t_ev, r_ps, r_ev, exp_in, exp_ok, comb_ok = (sem(n) for n in (
            "t_ps", "t_ev", "r_ps", "r_ev", "exp_in", "exp_ok", "comb_ok"))
        g_ps, u_ps, y_ps, gate_ok, hid_ok, y_ev, base_ok = (sem(n) for n in (
            "g_ps", "u_ps", "y_ps", "gate_ok", "hid_ok", "y_ev", "base_ok"))
        w_ok = sem("w_ok")
        routed = sem("routed")
        CHAIN = 18

        def need(eng, sm, b, per_row, c):
            value = b * per_row + c
            if not (isinstance(value, int) and value <= 0):
                eng.wait_ge(sm, value)

        def rows(engine, row):
            row(-1, 1, "lead")
            row(0, 0, "first")
            with engine.Fori(0, B // 2 - 1) as i:
                row(i * 2 + 1, 1, "")
                row(i * 2 + 2, 0, "")
            row(B - 1, 1, "last")

        def before(b, s, n):
            return (b, s, n - 1) if n else (b - 1, 1 - s, NEXP - 1)

        def buf(s, n):
            return (s * NEXP + n) % 2

        block = ctx.enter_context(nc.Block())

        @block.sync
        def _(sp):
            for dst, src in ((ident[:], w["ident"]), (wr[:], w["e_wr"]), (g2[:], w["g2"]), (r_bias[:], w["e_bias"].partition_broadcast(P)),
                             (rank[:], w["rank"].partition_broadcast(P))):
                sp.dma_start(dst, src).then_inc(const_in, 16)

            def store(b, s):
                sp.wait_ge(y_ev, b * NEXP + NEXP)
                sp.dma_start(out[b].rearrange("(t p) e -> p t e", p=P), y[s][:]).then_inc(stored, 16)

            def row(b, s, kind):
                if kind != "last":
                    need(sp, base_ok, b, 1, 1)
                    need(sp, nx_ok, b, 1, 1)
                    sp.dma_start(x1[1 - s][:], scr["x1"][b + 1]).then_inc(x_in, 16)
                if kind == "lead":
                    for dst, src in ((w1, w["e_w1"]), (w3, w["e_w3"]), (w2, w["e_w2"])):
                        sp.dma_start(dst[:], src).then_inc(weights_in, 16)
                if kind not in ("lead", "first"):
                    store(b - 1, 1 - s)
                    sp.wait_ge(stored, b * 16)
                if kind != "last":
                    sp.dma_start(y[1 - s][:], scr["y"][b + 1]).then_inc(y_in, 16)

            rows(sp, row)
            store(B - 1, 1)
            sp.wait_ge(stored, 16 * B)

        @block.tensor
        def _(pe):
            pe.wait_ge(const_in, N_IN)

            def up(b, s, n):
                e, k = FFN[n], buf(s, n)
                if n == 0:
                    need(pe, t_ev, b, 1, 1)
                need(pe, hid_ok, b, NEXP, n - 1)
                nc.tensor.matmul(b_g[k][:], w1[:, e, :], nx_t[s][:], start=True, stop=True).then_inc(g_ps, 1)
                nc.tensor.matmul(b_u[k][:], w3[:, e, :], nx_t[s][:], start=True, stop=True).then_inc(u_ps, 1)

            def down(b, s, n):
                e, k = FFN[n], buf(s, n)
                pe.wait_ge(hid_ok, b * NEXP + n + 1)
                need(pe, y_ev, b, NEXP, n - 1)
                for t in range(NT):
                    ins = nc.tensor.matmul(b_y[k][:, t * P:(t + 1) * P], hid[k][:, t * P:(t + 1) * P], w2[:, e, :],
                                           start=True, stop=True)
                ins.then_inc(y_ps, 1)

            def row(b, s, kind):
                if kind == "first":
                    pe.wait_ge(weights_in, 16 * 3)
                for n in range(NEXP):
                    if kind != "lead":
                        up(b, s, n)
                        if n or kind != "first":
                            down(*before(b, s, n))
                    if n == 2 and kind != "last":
                        pe.wait_ge(nx_ok, b + 2)
                        need(pe, t_ev, b, 1, 1)
                        for t in range(NT):
                            ins = nc.tensor.transpose(b_t[:, t * P:(t + 1) * P], nx[:, t, :], ident[:])
                        ins.then_inc(t_ps, 1)
                    if n == 3 and kind != "last":
                        pe.wait_ge(t_ev, b + 2)
                        need(pe, r_ev, b, 1, 1)
                        for t in range(NT):
                            ins = nc.tensor.matmul(b_r[:, t * NX:(t + 1) * NX], nx_t[1 - s][:, t * P:(t + 1) * P], wr[:],
                                                   start=True, stop=True)
                        ins.then_inc(r_ps, 1)

            rows(pe, row)
            down(B - 1, 1, NEXP - 1)

        @block.scalar
        def _(act):
            act.wait_ge(const_in, N_IN)

            def row(b, s, kind):
                for n in range(NEXP):
                    if n == 0 and kind != "last":
                        need(act, x_in, b, 16, 32)
                        need(act, ms_ok, b, 1, 1)
                        for t in range(NT):
                            need(act, sq_ok, b, NT, NT + t)
                            nc.scalar.activation(square[:], x1[1 - s][:, t, :], ACT.Square,
                                                 accum_out=mean_sq[:, t:t + 1]).then_inc(sq_ok, 1)
                    if n == 3 and kind != "last":
                        need(act, t_ps, b, 1, 2)
                        need(act, u_ps, b, NEXP, 0)
                        need(act, r_ps, b, 1, 0)
                        nc.scalar.activation(nx_t[1 - s][:], b_t[:], ACT.Copy, scale=g2[:]).then_inc(t_ev, 1)
                    if kind != "lead":
                        act.wait_ge(g_ps, b * NEXP + n + 1)
                        need(act, hid_ok, b, NEXP, n - 1)
                        nc.scalar.activation(gate[buf(s, n)][:], b_g[buf(s, n)][:], ACT.Silu).then_inc(gate_ok, 1)

            rows(act, row)

        @block.vector
        def _(v):
            nc.vector.memset(minus_half[:], -0.5).then_inc(const_ok, 1)
            nc.vector.memset(euler[:], math.e).then_inc(const_ok, 1)
            v.wait_ge(const_in, N_IN)

            def add(b, s, n):
                k = buf(s, n)
                v.wait_ge(y_ps, b * NEXP + n + 1)
                if n == 0:
                    v.wait_ge(base_ok, b + 1)
                    nc.vector.tensor_tensor(y[s][:].rearrange("p t e -> p (t e)"), y[s][:].rearrange("p t e -> p (t e)"),
                                            b_y[k][:], ALU.add).then_inc(y_ev, 1)
                    return
                v.wait_ge(y_ev, b * NEXP + n)
                if n == 1:
                    v.wait_ge(comb_ok, b + 1)
                e = FFN[n]
                for t in range(NT):
                    ins = nc.vector.scalar_tensor_tensor(y[s][:, t, :], b_y[k][:, t * P:(t + 1) * P],
                                                         comb[s][:, t, e:e + 1], y[s][:, t, :], ALU.mult, ALU.add)
                ins.then_inc(y_ev, 1)

            def chain(b, k):
                need(v, routed, b, CHAIN, CHAIN + k)

            def each(col):
                return col[:].rearrange("p (t o) -> p t o", o=1).to_broadcast([P, NT, NX])

            def by_rank():
                return rank[:].rearrange("p (o e) -> p o e", o=1).to_broadcast([P, NT, NX])

            def highest(b, k, values, best):
                chain(b, k)
                nc.vector.tensor_reduce(best[:], values[:], AX.X, ALU.max).then_inc(routed, 1)
                chain(b, k + 1)
                nc.vector.tensor_tensor(eq[:], values[:], each(best), ALU.is_equal).then_inc(routed, 1)

            def one_of(b, k, one):
                chain(b, k)
                nc.vector.tensor_tensor(eq[:], eq[:], by_rank(), ALU.mult).then_inc(routed, 1)
                chain(b, k + 1)
                nc.vector.tensor_reduce(key[:], eq[:], AX.X, ALU.max).then_inc(routed, 1)
                chain(b, k + 2)
                nc.vector.tensor_tensor(one[:], eq[:], each(key), ALU.is_equal).then_inc(routed, 1)

            def logits(b):
                need(v, r_ps, b, 1, 2)
                need(v, comb_ok, b, 1, 1)
                nc.vector.tensor_tensor(probs[:], b_r[:, 0:NT * NX].rearrange("p (t e) -> p t e", e=NX),
                                        r_bias[:].rearrange("p (o e) -> p o e", o=1).to_broadcast([P, NT, NX]),
                                        ALU.add).then_inc(r_ev, 1)
                need(v, r_ev, b, 1, 2)
                nc.vector.tensor_reduce(top[:], probs[:], AX.X, ALU.max).then_inc(routed, 1)
                chain(b, 1)
                nc.vector.tensor_tensor(probs[:], probs[:], each(top), ALU.subtract).then_inc(exp_in, 1)

            def first_pick(b):
                need(v, exp_ok, b, 2, 3)
                nc.vector.tensor_reduce(total[:], probs[:], AX.X, ALU.add).then_inc(routed, 1)
                chain(b, 2)
                nc.vector.reciprocal(total[:], total[:]).then_inc(routed, 1)
                chain(b, 3)
                nc.vector.tensor_tensor(probs[:], probs[:], each(total), ALU.mult).then_inc(routed, 1)
                highest(b, 4, probs, top0)

            def second_pick(b):
                one_of(b, 6, one0)
                chain(b, 9)
                nc.vector.scalar_tensor_tensor(rest[:], one0[:], TAKEN, probs[:], ALU.mult, ALU.add).then_inc(routed, 1)
                highest(b, 10, rest, top1)

            def difference(b):
                one_of(b, 12, one1)
                nc.vector.tensor_tensor(w_1[:], top1[:], top0[:], ALU.subtract).then_inc(exp_in, 1)

            def weights(b, s):
                need(v, exp_ok, b, 2, 4)
                nc.vector.tensor_scalar(w_0[:], w_1[:], 1.0, None, ALU.add).then_inc(routed, 1)
                chain(b, 16)
                nc.vector.reciprocal(w_0[:], w_0[:]).then_inc(routed, 1)
                chain(b, 17)
                nc.vector.tensor_tensor(w_1[:], w_1[:], w_0[:], ALU.mult)
                nc.vector.tensor_tensor(one0[:], one0[:], each(w_0), ALU.mult).then_inc(routed, 1)
                chain(b, 18)
                nc.vector.tensor_tensor(one1[:], one1[:], each(w_1), ALU.mult).then_inc(w_ok, 1)
                need(v, w_ok, b, 1, 2)
                need(v, y_ev, b, NEXP, 0)
                nc.vector.tensor_tensor(comb[1 - s][:], one0[:], one1[:], ALU.add).then_inc(comb_ok, 1)

            def row(b, s, kind):
                for n in range(NEXP):
                    if kind != "lead":
                        q = b * NEXP + n + 1
                        v.wait_ge(gate_ok, q)
                        v.wait_ge(u_ps, q)
                        need(v, y_ps, b, NEXP, n - 1)
                        k = buf(s, n)
                        nc.vector.tensor_tensor(hid[k][:], gate[k][:], b_u[k][:], ALU.mult).then_inc(hid_ok, 1)
                        if n or kind != "first":
                            add(*before(b, s, n))
                    if kind == "last":
                        continue
                    if n == 0:
                        need(v, sq_ok, b, NT, 2 * NT)
                        need(v, nx_ok, b, 1, 1)
                        nc.vector.tensor_scalar(rms[:], mean_sq[:], 1.0 / E, RMS_EPS, ALU.mult, ALU.add).then_inc(ms_ok, 1)
                    if n == 1:
                        need(v, rms_ok, b, 1, 2)
                        need(v, t_ps, b, 1, 1)
                        for t in range(NT):
                            ins = nc.vector.tensor_scalar(nx[:, t, :], x1[1 - s][:, t, :], rms[:, t:t + 1], None, ALU.mult)
                        ins.then_inc(nx_ok, 1)
                    if n == 4:
                        logits(b)
                    if n == 6:
                        first_pick(b)
                    if n == 7:
                        second_pick(b)
                        difference(b)
                    if n == 8:
                        weights(b, s)

            rows(v, row)
            add(B - 1, 1, NEXP - 1)

        @block.gpsimd
        def _(g):
            g.wait_ge(const_ok, 2)

            def row(b, s, kind):
                if kind == "last":
                    return
                need(g, ms_ok, b, 1, 2)
                nc.gpsimd.tensor_tensor(rms[:], rms[:], minus_half[:].to_broadcast([P, NT]), ALU.pow).then_inc(rms_ok, 1)
                need(g, y_in, b, 16, 32)
                need(g, x_in, b, 16, 32)
                nc.gpsimd.tensor_tensor(y[1 - s][:], y[1 - s][:], x1[1 - s][:], ALU.add).then_inc(base_ok, 1)
                flat = probs[:].rearrange("p t e -> p (t e)")
                need(g, exp_in, b, 2, 3)
                nc.gpsimd.tensor_tensor(flat, euler[:].to_broadcast([P, NT * NX]), flat, ALU.pow).then_inc(exp_ok, 1)
                need(g, exp_in, b, 2, 4)
                nc.gpsimd.tensor_tensor(w_1[:], euler[:].to_broadcast([P, NT]), w_1[:], ALU.pow).then_inc(exp_ok, 1)

            rows(g, row)


def program(nc, a, out):
    scr = {
        "y": nc.dram_tensor("scr_y", (B, P, NT, E), F32, kind="Internal").ap(),
        "xn": nc.dram_tensor("scr_xn", (B, P, NT, E), F32, kind="Internal").ap(),
        "x1": nc.dram_tensor("scr_x1", (B, P, NT, E), F32, kind="Internal").ap(),
        "v": nc.dram_tensor("scr_v", (B, P, NT, E), F32, kind="Internal").ap(),
        "parts": nc.dram_tensor("scr_parts", (B, 3, PARTS, P, S), BF16, kind="Internal").ap(),
        "qr": nc.dram_tensor("scr_qr", (B * NT + 1, P, H * FAR), F32, kind="Internal").ap(),
        "qr0": nc.dram_tensor("scr_qr0", (B, P, NT, H), F32, kind="Internal").ap(),
    }
    scr["probs"] = nc.dram_tensor("scr_probs", (2 * (MARGIN + P * H * WIDE),), F32, kind="Internal").ap()
    prepare(nc, a["x"], a, scr, a["ident"])
    attend(nc, a, scr)
    mix(nc, a, scr)
    experts(nc, a, scr, out)


def lay_out(inputs):
    import numpy as np

    g = {k: np.asarray(v) for k, v in inputs.items()}
    f = np.float32
    order = np.array([(2 * half + par) * HD + d for par in range(2) for d in range(HD) for half in range(G)])
    wide = np.array([d for par in range(2) for d in range(HD) for half in range(G)])
    rel_k, rel_v = g["L0_attn_rel_k"], g["L0_attn_rel_v"]
    rel = np.zeros((P, H, FAR + 1), f)
    for p in range(P):
        rel[p, order[p] // HD] = rel_k[:, wide[p]]
    key = np.arange(P)[:, None]
    v_edges = np.stack([np.where(key < edge, np.tile(rel_v[0], H), np.tile(rel_v[FAR], H)) for edge in EDGES], 1)
    feat_w, feat_last = np.zeros((P, FC, P), f), np.zeros((P, FC, P), f)
    for n in range(H * NF):
        h, r = divmod(n, NF)
        feat_w[n % P, n // P, h * HD:(h + 1) * HD] = rel_v[r]
        feat_last[n % P, n // P, h * HD:(h + 1) * HD] = rel_v[FAR]
    place = np.arange(WIN)[None] - key % QBLK
    keep = (np.arange(QBLK)[None] - (QBLK - 1) >= -(key % QBLK)).astype(f)
    first = {n: np.concatenate([g["L0_ffn_e" + n], g["L0_ffn_s" + n][None]]).transpose(2, 0, 1)
             for n in ("W1", "W2", "W3")}
    return {
        "x": g["L0_attn_hidden_states"],
        "ident": np.eye(P, dtype=f),
        "wq": g["L0_attn_Wq"][order].T, "wk": g["L0_attn_Wk"][order].T, "wv": g["L0_attn_Wv"].T,
        "qk_bias": np.stack([g["L0_attn_bq"][order], g["L0_attn_bk"][order], rel_k[0][wide], rel_k[FAR][wide]], 1),
        "rel": rel,
        "bo": g["L0_attn_bo"],
        "wo": g["L0_attn_Wo"].T, "bv": g["L0_attn_bv"],
        "m_wq": g["L0_ffn_Wq"].T, "m_wk": np.tile(g["L0_ffn_Wkc"].T, (1, H2)), "m_wv": g["L0_ffn_Wvc"].T,
        "m_wo": g["L0_ffn_Wo"].T, "g1": g["L0_ffn_g1"][:, None], "g2": g["L0_ffn_g2"][:, None],
        "e_w1": first["W1"], "e_w3": first["W3"], "e_w2": first["W2"],
        "e_wr": g["L0_ffn_Wr"].T, "e_bias": g["L0_ffn_expert_bias"], "rank": np.arange(NX, 0, -1).astype(f),
        "v_edges": v_edges, "feat_w": feat_w, "feat_last": feat_last, "keep": keep,
        "band": ((place >= 0) & (place < FAR)).astype(f), "beyond": (place[:, :QBLK - 1] < 0).astype(f),
    }


def kernel(**inputs):
    import numpy as np
    import concourse.bacc as bacc
    from concourse.bass_utils import run_bass_kernel_spmd

    nc = bacc.Bacc("TRN2", target_bir_lowering=False, num_devices=1)
    arrays = {"in_" + k: np.ascontiguousarray(v) for k, v in lay_out(inputs).items()}
    aps = {k[3:]: nc.dram_tensor(k, v.shape, mybir.dt.from_np(v.dtype), kind="ExternalInput").ap()
           for k, v in arrays.items()}
    out = nc.dram_tensor("out_0", (B, S, E), F32, kind="ExternalOutput").ap()
    program(nc, aps, out)
    return run_bass_kernel_spmd(nc, [arrays], core_ids=[0]).results[0]["out_0"]
```
